# Optimizing a Trainium2 kernel written in Bass

```python
import numpy as np
import jax
import jax.numpy as jnp

def _softmax(x, axis=-1):
    return jax.nn.softmax(x, axis=axis)

def _gelu(x):
    return jax.nn.gelu(x, approximate=True)

def _silu(x):
    return jax.nn.silu(x)

def _sigmoid(x):
    return jax.nn.sigmoid(x)

def _layernorm(x, axis=-1, eps=1e-05):
    m = jnp.mean(x, axis=axis, keepdims=True)
    v = jnp.var(x, axis=axis, keepdims=True)
    return (x - m) / jnp.sqrt(v + eps)

def _scatter_add(tgt, idx, src, axis=0):
    return tgt.at[idx].add(src)

def _segment_sum(src, seg, n):
    return jax.ops.segment_sum(src, seg, n)
kernel_name = 'mk_seq_preln_d1_jaxref_r2_430cbf'

def setup_inputs(seed: int=0):
    np.random.seed(seed)
    _w = jnp.asarray

    def _L0_attn_setup():
        import jax, jax.numpy as jnp
        import numpy as np
        B, T, D, H = (4, 1024, 512, 16)
        HD = D // H
        EPS = 1e-06

        def _phi(x):
            return jax.nn.elu(x) + 1.0

        def _linear_attn(x, Wq, bq, Wk, bk, Wv, bv, Wo, bo):
            b, t, d = x.shape

            def proj(W, bias):
                y = x @ W.T + bias
                return y.reshape(b, t, H, HD).transpose(0, 2, 1, 3)
            qp = _phi(proj(Wq, bq))
            kp = _phi(proj(Wk, bk))
            v = proj(Wv, bv)
            q_tm = qp.transpose(2, 0, 1, 3)
            k_tm = kp.transpose(2, 0, 1, 3)
            v_tm = v.transpose(2, 0, 1, 3)
            kv0 = jnp.zeros((b, H, HD, HD), dtype=x.dtype)
            ks0 = jnp.zeros((b, H, HD), dtype=x.dtype)

            def step(carry, inp):
                kv, ksum = carry
                kt, vt, qt = inp
                kv = kv + jnp.einsum('bhd,bhe->bhde', kt, vt)
                ksum = ksum + kt
                num = jnp.einsum('bhd,bhde->bhe', qt, kv)
                den = jnp.einsum('bhd,bhd->bh', qt, ksum)[..., None] + EPS
                return ((kv, ksum), num / den)
            _, out_tm = jax.lax.scan(step, (kv0, ks0), (k_tm, v_tm, q_tm))
            out = out_tm.transpose(1, 0, 2, 3).reshape(b, t, d)
            return out @ Wo.T + bo
        key = jax.random.key(seed)
        ks = jax.random.split(key, 9)
        s = 1.0 / np.sqrt(D)
        return {'x': jax.random.normal(ks[0], (B, T, D), dtype=jnp.float32), 'Wq': jax.random.normal(ks[1], (D, D), dtype=jnp.float32) * s, 'bq': jnp.zeros((D,), dtype=jnp.float32), 'Wk': jax.random.normal(ks[2], (D, D), dtype=jnp.float32) * s, 'bk': jnp.zeros((D,), dtype=jnp.float32), 'Wv': jax.random.normal(ks[3], (D, D), dtype=jnp.float32) * s, 'bv': jnp.zeros((D,), dtype=jnp.float32), 'Wo': jax.random.normal(ks[4], (D, D), dtype=jnp.float32) * s, 'bo': jnp.zeros((D,), dtype=jnp.float32)}
    _L0_attn_in = _L0_attn_setup()

    def _L0_ffn_setup():
        import jax, jax.numpy as jnp
        import numpy as np
        CAPACITY_FACTOR = 1.25
        key = jax.random.key(seed)
        ks = jax.random.split(key, 6)
        B, S, H, E = (4, 2048, 512, 8)
        scale = 1.0 / np.sqrt(H)
        return {'tokens': jax.random.normal(ks[0], (B, S, H), dtype=jnp.float32), 'gate_w': jax.random.normal(ks[1], (E, H), dtype=jnp.float32) * scale, 'w1': jax.random.normal(ks[2], (E, H, H), dtype=jnp.float32) * scale, 'b1': jax.random.normal(ks[3], (E, H), dtype=jnp.float32) * 0.01, 'w2': jax.random.normal(ks[4], (E, H, H), dtype=jnp.float32) * scale, 'b2': jax.random.normal(ks[5], (E, H), dtype=jnp.float32) * 0.01}
    _L0_ffn_in = _L0_ffn_setup()
    _d = {'L0_attn_x': _L0_attn_in['x'], 'L0_attn_Wq': _L0_attn_in['Wq'], 'L0_attn_bq': _L0_attn_in['bq'], 'L0_attn_Wk': _L0_attn_in['Wk'], 'L0_attn_bk': _L0_attn_in['bk'], 'L0_attn_Wv': _L0_attn_in['Wv'], 'L0_attn_bv': _L0_attn_in['bv'], 'L0_attn_Wo': _L0_attn_in['Wo'], 'L0_attn_bo': _L0_attn_in['bo'], 'L0_ffn_gate_w': _L0_ffn_in['gate_w'], 'L0_ffn_w1': _L0_ffn_in['w1'], 'L0_ffn_b1': _L0_ffn_in['b1'], 'L0_ffn_w2': _L0_ffn_in['w2'], 'L0_ffn_b2': _L0_ffn_in['b2']}
    _x0 = _d['L0_attn_x']
    _d['L0_attn_x'] = jax.random.normal(jax.random.fold_in(jax.random.key(seed), 1), (16, 1024, 512), dtype=_x0.dtype)
    del _x0
    return _d

def reference(L0_attn_x, L0_attn_Wq, L0_attn_bq, L0_attn_Wk, L0_attn_bk, L0_attn_Wv, L0_attn_bv, L0_attn_Wo, L0_attn_bo, L0_ffn_gate_w, L0_ffn_w1, L0_ffn_b1, L0_ffn_w2, L0_ffn_b2):

    def _L0_attn_ref(x, Wq, bq, Wk, bk, Wv, bv, Wo, bo):
        import jax, jax.numpy as jnp
        import numpy as np
        B, T, D, H = (4, 1024, 512, 16)
        HD = D // H
        EPS = 1e-06

        def _phi(x):
            return jax.nn.elu(x) + 1.0

        def _linear_attn(x, Wq, bq, Wk, bk, Wv, bv, Wo, bo):
            b, t, d = x.shape

            def proj(W, bias):
                y = x @ W.T + bias
                return y.reshape(b, t, H, HD).transpose(0, 2, 1, 3)
            qp = _phi(proj(Wq, bq))
            kp = _phi(proj(Wk, bk))
            v = proj(Wv, bv)
            q_tm = qp.transpose(2, 0, 1, 3)
            k_tm = kp.transpose(2, 0, 1, 3)
            v_tm = v.transpose(2, 0, 1, 3)
            kv0 = jnp.zeros((b, H, HD, HD), dtype=x.dtype)
            ks0 = jnp.zeros((b, H, HD), dtype=x.dtype)

            def step(carry, inp):
                kv, ksum = carry
                kt, vt, qt = inp
                kv = kv + jnp.einsum('bhd,bhe->bhde', kt, vt)
                ksum = ksum + kt
                num = jnp.einsum('bhd,bhde->bhe', qt, kv)
                den = jnp.einsum('bhd,bhd->bh', qt, ksum)[..., None] + EPS
                return ((kv, ksum), num / den)
            _, out_tm = jax.lax.scan(step, (kv0, ks0), (k_tm, v_tm, q_tm))
            out = out_tm.transpose(1, 0, 2, 3).reshape(b, t, d)
            return out @ Wo.T + bo
        return _linear_attn(x, Wq, bq, Wk, bk, Wv, bv, Wo, bo)

    def _L0_ffn_ref(tokens, gate_w, w1, b1, w2, b2):
        import jax, jax.numpy as jnp
        import numpy as np
        CAPACITY_FACTOR = 1.25
        B, S, H = tokens.shape
        E = gate_w.shape[0]
        N = B * S
        cap = int(CAPACITY_FACTOR * N / E)
        x = tokens.reshape(N, H)
        probs = jax.nn.softmax(x @ gate_w.T, axis=-1)
        top2_w, top2_idx = jax.lax.top_k(probs, 2)
        a_e = top2_idx.reshape(-1)
        a_w = top2_w.reshape(-1)
        tok_id = jnp.arange(2 * N) // 2
        counts = jnp.bincount(a_e, length=E)
        keep = counts <= cap
        valid = keep[a_e]
        onehot = jax.nn.one_hot(a_e, E, dtype=jnp.int32)
        pos = jnp.take_along_axis(jnp.cumsum(onehot, axis=0) - 1, a_e[:, None], axis=1)[:, 0]
        p = jnp.where(valid, jnp.minimum(pos, cap - 1), cap)
        x_a = x[tok_id]
        buf = jnp.zeros((E, cap + 1, H), dtype=x.dtype).at[a_e, p].set(x_a)
        h = jax.nn.silu(jnp.einsum('ech,efh->ecf', buf, w1) + b1[:, None, :])
        y = jnp.einsum('ecf,egf->ecg', h, w2) + b2[:, None, :]
        contrib = y[a_e, p] * (a_w * valid.astype(x.dtype))[:, None]
        out = contrib.reshape(N, 2, H).sum(axis=1)
        return out.reshape(B, S, H)
    x = L0_attn_x
    x = x + _L0_attn_ref(_layernorm(x, axis=-1), L0_attn_Wq, L0_attn_bq, L0_attn_Wk, L0_attn_bk, L0_attn_Wv, L0_attn_bv, L0_attn_Wo, L0_attn_bo)
    x = x + _L0_ffn_ref(_layernorm(x, axis=-1), L0_ffn_gate_w, L0_ffn_w1, L0_ffn_b1, L0_ffn_w2, L0_ffn_b2)
    return x

_drawn_inputs = setup_inputs


def setup_inputs(seed=0):
    import zlib

    import numpy as np

    out = dict(_drawn_inputs(seed))
    spreads = {'L0_attn_bq': (0.0, 0.8),
     'L0_attn_bk': (0.0, 0.8),
     'L0_attn_bv': (0.0, 0.1),
     'L0_attn_bo': (0.0, 0.1)}
    factors = {'L0_attn_Wq': 8.0, 'L0_attn_Wk': 4.611}
    for name, (base, spread) in spreads.items():
        noise = np.random.default_rng([zlib.crc32(name.encode()), seed]).standard_normal(out[name].shape)
        drawn = base * np.exp(spread * noise) if base else spread * noise
        out[name] = jnp.asarray(drawn.astype(out[name].dtype))
    for name, factor in factors.items():
        out[name] = (out[name] * factor).astype(out[name].dtype)
    return out
```

```python
from contextlib import ExitStack

import numpy as np

import concourse.bass as bass
import concourse.mybir as mybir

F32 = mybir.dt.float32
F32R = mybir.dt.float32r
I32 = mybir.dt.int32
ALU = mybir.AluOpType
ACT = mybir.ActivationFunctionType
AXX = mybir.AxisListType.X

P = 128
HEADS, HD = 16, 32
D = HEADS * HD
KD = D // P
HPG = P // HD
TPB = 4
BT = TPB * P
E = 8
EH = E // 2
DH = D // 2
HW = DH + EH
LN_EPS = 1e-5
DEN_EPS = 1e-6
CAPACITY_FACTOR = 1.25
CREDIT = 2
NBANK = 4

CHUNKS = {(0, 0): [("Q", 0)], (0, 1): [("K", 0)], (0, 2): [("Q", 1)],
          (1, 0): [("K", 1)], (1, 1): [("Q", 2)], (1, 2): [("K", 2)],
          (2, 0): [("Q", 3)], (2, 1): [("K", 3)], (2, 2): [("V", 0)],
          (3, 0): [("V", 1)], (3, 1): [("V", 2)], (3, 2): [("V", 3)]}


def ring_uses():
    uses = []
    for c in range(TPB):
        last = c == TPB - 1
        uses += [("DEN", 0)] * last + [("T", c)] + [("X", 0)] * last
        for n in range(3):
            if last and n == 1:
                uses += [("R", 0), ("R", 1)]
            for kind, j in CHUNKS[c, n]:
                uses += [(kind, j)] if kind != "V" else [("V", (j, 0)), ("V", (j, 1))]
            if last and n == 1:
                uses += [("R", 2), ("R", 3), ("X", 2)]
            elif last:
                uses += [("X", n + 1)]
        uses += [("O", (c, 0)), ("O", (c, 1))]
    return uses


USES = ring_uses()
BANK = {u: n % NBANK for n, u in enumerate(USES)}


def part_of(kind):
    return "attn" if kind in ("T", "O") else "turn" if kind == "X" else "proj"


def uses_of(parts):
    return [u for u in USES if part_of(u[0]) in parts]


def per_bank(parts):
    return [sum(BANK[u] == k for u in uses_of(parts)) for k in range(NBANK)]


ALL = ("attn", "proj", "turn")


class Step:

    def __init__(self, i, off, parts, base):
        self.i, self.off, self.parts, self.base = i, off, parts, base

    def has(self, part):
        return part in self.parts

    def lin(self, k, off, c=0):
        return self.i * (2 * k) + (k * off + c)

    def before(self, k):
        return self.base[k] if isinstance(self.i, int) else self.i * (2 * per_bank(ALL)[k]) + self.base[k]

    def use(self, u):
        k = BANK[u]
        rank = sum(BANK[v] == k for v in uses_of(self.parts)[:uses_of(self.parts).index(u)])
        n = self.base[k] + rank
        if isinstance(self.i, int):
            return k, n
        return k, self.i * (2 * per_bank(ALL)[k]) + n



class Sem:

    def __init__(self, handle, credit=0):
        self.handle, self.credit = handle, credit


def attention(nc, ctx, io, n_blocks, keepers):
    z_all, ident, ones = keepers["z_all"], keepers["ident"], keepers["ones"]
    x_t = io["x"].rearrange("(n p) d -> n p d", p=P)
    out_t = io["out"].rearrange("(n p) d -> n p d", p=P)

    def sb(name, shape, dt=F32):
        return ctx.enter_context(nc.sbuf_tensor(name, shape, dt))[:]

    def ps(name, shape):
        return ctx.enter_context(nc.psum_tensor(name, shape, F32))[:]

    def sem(name, credit=0):
        return Sem(ctx.enter_context(nc.semaphore(name)), credit)

    w_q = [sb(f"wq_{h}", [P, KD, D], F32R) for h in ("hi", "lo")]
    w_k = [sb(f"wk_{h}", [P, KD, D], F32R) for h in ("hi", "lo")]
    w_v = [sb(f"wv_{h}", [P, KD, 2, HW], F32R) for h in ("hi", "lo")]
    w_o = [sb(f"wo_{h}", [P, KD, 2, HW], F32R) for h in ("hi", "lo")]
    x_in = sb("x_in", [P, TPB, D])
    x_norm = sb("x_norm", [P, 2, D])
    xt = [sb(f"xt_{h}", [P, KD, BT], F32R) for h in ("hi", "lo")]
    q_raw = sb("q_raw", [P, KD, BT])
    q_div = sb("q_div", [P, KD, BT])
    q_hl = sb("q_hl", [P, KD, 2, P], F32R)
    k_hl = sb("k_hl", [P, KD, 2, P], F32R)
    q_diag = sb("q_diag", [P, KD, 2, HPG, P], F32R)
    k_t = sb("k_t", [P, 2, KD, BT])
    k_sum = sb("k_sum", [P, KD, BT])
    k_carry = sb("k_carry", [P, KD])
    e_tmp = sb("e_tmp", [P, 2, BT])
    v_tok = sb("v_tok", [P, TPB, D])
    k_tok = sb("k_tok", [P, D])
    s_mask = sb("s_mask", [P, 2, HPG, P])
    kv_diag = sb("kv_diag", [P, KD, P])
    o_t = [sb(f"o_{h}", [P, KD, P], F32R) for h in ("hi", "lo")]
    res = sb("res", [P, 2, D])
    den = sb("den", [P, BT])
    rden = [sb(f"rden_{h}", [P, BT], F32R) for h in ("hi", "lo")]
    causal = sb("causal", [P, P])
    diag_blocks = sb("diag_blocks", [P, P])
    head_cols = sb("head_cols", [P, HD])
    spread = sb("spread", [P, KD, P], F32R)
    bias = sb("bias", [P, 2, KD])
    bias_n = sb("bias_n", [P, 2, KD])
    bv_row = sb("bv_row", [P, D])
    bo_row = sb("bo_row", [P, D])
    bo_col = sb("bo_col", [P, KD])
    gw = sb("gw", [P, KD, E])
    gw_bo = sb("gw_bo", [P, KD, E])
    g_sum = sb("g_sum", [P, E])
    g_bo = sb("g_bo", [P, E])
    stats = sb("stats", [P, TPB, 6])
    mv0 = sb("mv0", [P, 2, TPB, 2])
    var0 = sb("var0", [P, 2, TPB])
    rstd0 = sb("rstd0", [P, 2, TPB])
    std0 = sb("std0", [P, TPB])
    stats1 = sb("stats1", [P, TPB, 6])
    mv1 = sb("mv1", [P, TPB, 2])
    var1 = sb("var1", [P, TPB])
    rstd1 = sb("rstd1", [P, TPB])
    gate_x = sb("gate_x", [P, 2, TPB, E])
    gate_o = sb("gate_o", [P, TPB, E])
    z_a = sb("z_a", [P, TPB, E])
    z_b = sb("z_b", [P, TPB, E])
    neg_half = sb("neg_half", [P, TPB])

    ring = ps("ring", [P, NBANK, 512])
    s_ps = ps("s_ps", [P, 2, HPG, P])
    num_ps = ps("num_ps", [P, KD, P])
    kv_ps = ps("kv_ps", [P, KD, P])

    def over(ap, n):
        ap = ap if len(ap.shape) == 3 else ap.unsqueeze(2)
        return ap.to_broadcast([ap.shape[0], ap.shape[1], n])

    def repeat(ap, n):
        return ap.unsqueeze(1).to_broadcast([ap.shape[0], n, ap.shape[1]])

    spread_f = e_tmp[:, 0].rearrange("p (g m) -> p g m", g=KD)

    stages = {"wq_t": q_raw, "wk_t": q_div, "wv_t": k_t[:, 0], "wo_t": k_t[:, 1],
              "wo": k_sum}
    w_load = {name: sem(f"load_{name}") for name in stages}
    small_load, pool_set, dve_set = sem("small_load"), sem("pool_set"), sem("dve_set")
    act_hi, pe_gate, dve_gate = sem("act_hi"), sem("pe_gate"), sem("dve_gate")
    splits = [("wq_t", w_q), ("wk_t", w_k), ("wv_t", w_v), ("wo_t", w_o)]
    N_SMALL = 7

    def halves(ap):
        return ap.rearrange("p k h w -> p (k h) w")[:, :, 0:DH]

    def gates_of(ap):
        return ap.rearrange("p k h w -> p (k h) w")[:, :, DH:HW]

    with nc.Block() as block:
        @block.sync
        def _(sp):
            for name, stage in stages.items():
                sp.dma_start(stage, io[name].rearrange("(k p) d -> p k d", p=P)
                             ).then_inc(w_load[name].handle, 16)

        @block.scalar
        def _(act):
            with nc.allow_non_contiguous_dma("a few columns of biases"):
                for dst, src in ((bias[:, 0], io["bq"]), (bias[:, 1], io["bk"]), (bo_col, io["bo"])):
                    act.dma_start(dst, src.rearrange("(k p) -> p k", p=P)).then_inc(small_load.handle, 16)
                act.dma_start(gw, io["gate"].rearrange("(k p) e -> p k e", p=P)
                              ).then_inc(small_load.handle, 16)
            for dst, src in ((bv_row, io["bv"]), (bo_row, io["bo"])):
                act.dma_start(dst, src.rearrange("(a d) -> a d", a=1).to_broadcast([P, D])
                              ).then_inc(small_load.handle, 16)
            for name, w in splits:
                act.wait_ge(w_load[name].handle, 16)
                if w in (w_q, w_k):
                    act.activation(w[0], stages[name], ACT.Copy).then_inc(act_hi.handle, 1)
                else:
                    act.activation(halves(w[0]), stages[name].rearrange("p k (h d) -> p (k h) d", h=2),
                                   ACT.Copy).then_inc(act_hi.handle, 1)

        @block.gpsimd
        def _(pool):
            n = [0]

            def link(ins):
                n[0] += 1
                ins.then_inc(pool_set.handle, 1)
                pool.wait_ge(pool_set.handle, n[0])

            link(pool.memset(q_diag.bitcast(F32), 0.0))
            link(pool.memset(neg_half, -0.5))
            link(pool.memset(ones, 1.0))
            link(pool.memset(ident, 0.0))
            link(pool.affine_select(out=ident, in_=ident, compare_op=ALU.not_equal, fill=1.0, base=0,
                                    pattern=[[-1, P]], channel_multiplier=1))
            link(pool.memset(causal, 1.0))
            link(pool.affine_select(out=causal, in_=causal, compare_op=ALU.is_ge, fill=0.0, base=0,
                                    pattern=[[1, P]], channel_multiplier=-1))
            link(pool.memset(diag_blocks, 1.0))
            v = diag_blocks.rearrange("p (j e) -> p j e", j=HPG)
            link(pool.affine_select(out=v, in_=v, compare_op=ALU.is_ge, fill=0.0, base=0,
                                    pattern=[[-HD, HPG], [0, HD]], channel_multiplier=1))
            link(pool.affine_select(out=v, in_=v, compare_op=ALU.is_ge, fill=0.0, base=HD - 1,
                                    pattern=[[HD, HPG], [0, HD]], channel_multiplier=-1))
            link(pool.memset(head_cols, 0.0))
            link(pool.tensor_copy(head_cols[:, 0:HPG], v[:, :, 0]))
            s = spread_f
            link(pool.memset(s, 0.0))
            v = s.rearrange("p g (j e) -> p g j e", j=HPG)
            link(pool.affine_select(out=v, in_=v, compare_op=ALU.not_equal, fill=1.0, base=0,
                                    pattern=[[-HD, KD], [-1, HPG], [0, HD]], channel_multiplier=1))

        @block.vector
        def _(dve):
            n = [0]

            def link(ins):
                n[0] += 1
                ins.then_inc(dve_set.handle, 1)
                dve.wait_ge(dve_set.handle, n[0])

            dve.wait_ge(small_load.handle, 16 * 6)
            link(dve.tensor_scalar(bias_n, bias, -1.0, None, ALU.mult))
            link(dve.tensor_scalar(bias, bias, 1.0, None, ALU.add))
            link(dve.tensor_tensor(gw_bo, gw, over(bo_col, E), ALU.mult))
            for m, (name, w) in enumerate(splits):
                dve.wait_ge(act_hi.handle, m + 1)
                if w in (w_q, w_k):
                    link(dve.tensor_tensor(w[1], stages[name], w[0].bitcast(F32), ALU.subtract))
                else:
                    link(dve.tensor_tensor(halves(w[1]), stages[name].rearrange("p k (h d) -> p (k h) d", h=2),
                                           halves(w[0].bitcast(F32)), ALU.subtract))
            gates = gw.rearrange("p k (h e) -> p (k h) e", h=2)
            link(dve.tensor_copy(gates_of(w_v[0]), gates))
            link(dve.tensor_tensor(gates_of(w_v[1]), gates, gates_of(w_v[0].bitcast(F32)), ALU.subtract))
            dve.wait_ge(pe_gate.handle, 1)
            gates = ring[:, 0, 0:KD * E].rearrange("p (k e) -> p k e", e=EH)
            link(dve.tensor_copy(gates_of(w_o[0]), gates))
            link(dve.tensor_tensor(gates_of(w_o[1]), gates, gates_of(w_o[0].bitcast(F32)), ALU.subtract))
            link(dve.tensor_copy(g_sum, ring[:, 1, 0:E]))
            link(dve.tensor_copy(g_bo, ring[:, 1, E:2 * E]))
            dve.wait_ge(pool_set.handle, 14)
            link(dve.tensor_copy(spread, spread_f))

        @block.tensor
        def _(pe):
            pe.wait_ge(small_load.handle, 16 * 6)
            pe.wait_ge(w_load["wo"].handle, 16)
            pe.wait_ge(pool_set.handle, 3)
            pe.wait_ge(dve_set.handle, 3)
            for k in range(KD):
                for f in range(KD):
                    pe.matmul(ring[:, 0, k * E:(k + 1) * E], stages["wo"][:, f, k * P:(k + 1) * P],
                              gw[:, f, :], start=f == 0, stop=f == KD - 1)
            for m, g in enumerate((gw, gw_bo)):
                for f in range(KD):
                    mm = pe.matmul(ring[:, 1, m * E:(m + 1) * E], ones, g[:, f, :],
                                   start=f == 0, stop=f == KD - 1)
            mm.then_inc(pe_gate.handle, 1)

    nc.all_engine_barrier()

    full = [sem(f"ring_full{k}") for k in range(NBANK)]
    free = [sem(f"ring_free{k}", CREDIT) for k in range(NBANK)]
    x_load = [sem(f"x_load{c}") for c in range(TPB)]
    res_load = [sem(f"res_load{n}") for n in range(2)]
    hi_parts, lo_parts = sem("hi_parts"), sem("lo_parts")
    diag_load = [sem(f"diag_load{n}") for n in range(2)]
    stored = [sem(f"stored{n}", 16) for n in range(2)]
    x_stat, x_aggr, x_var, x_rstd, x_normed = (sem("x_stat"), sem("x_aggr"), sem("x_var"),
                                               sem("x_rstd"), sem("x_normed"))
    xt_hi, phi_relu, phi_exp = sem("xt_hi"), sem("phi_relu"), sem("phi_exp")
    k_scan, k_carried, prod = sem("k_scan"), sem("k_carried"), sem("prod")
    den_rec, rden_hi, rden_lo = sem("den_rec"), sem("rden_hi"), sem("rden_lo")
    scored, masked, summed = sem("scored", CREDIT), sem("masked", CREDIT), sem("summed")
    kv_done, kv_masked = sem("kv_done"), sem("kv_masked")
    o_hi, o_lo, res_bias = sem("o_hi"), sem("o_lo", CREDIT), sem("res_bias")
    x1_stat, x1_aggr = sem("x1_stat", CREDIT), sem("x1_aggr")
    gx_link, gx_done, z_link, z_done = sem("gx_link"), sem("gx_done"), sem("z_link"), sem("z_done", CREDIT)

    waited = {e.engine: sem(f"waited_{n}") for n, e in enumerate((nc.sync, nc.vector, nc.gpsimd))}

    def wait(eng, s, n):
        n = n + s.credit
        if not isinstance(n, int) or n > 0:
            eng.wait_ge(s.handle, n)
            if eng.engine == nc.sync.engine and not isinstance(n, int):
                eng.sem_inc(waited[eng.engine].handle, 1)

    def wait_alone(eng, s, n):
        wait(eng, s, n)
        if eng.engine != nc.sync.engine:
            eng.sem_inc(waited[eng.engine].handle, 1)

    def give(eng, *sems):
        for s in sems:
            eng.sem_inc(s.handle, s.credit)

    def wait_full(eng, st, u):
        k, n = st.use(u)
        wait(eng, full[k], n + 1)
        return ring[:, k, :]

    def wait_free(eng, st, u):
        k, n = st.use(u)
        wait(eng, free[k], n + 1)

    def wait_step_before(eng, st, *kinds):
        for k in sorted({BANK[u] for u in USES if u[0] in kinds}):
            wait(eng, free[k], st.before(k))

    def claim(pe, st, u):
        k, n = st.use(u)
        wait(pe, free[k], n)
        return ring[:, k, :]

    def done(sem_, ins):
        ins.then_inc(sem_.handle, 1)

    def filled(u, ins):
        done(full[BANK[u]], ins)

    def release(u, ins):
        done(free[BANK[u]], ins)

    loops = (n_blocks - 2) // 2
    base_m1 = per_bank(("turn",))
    base_0 = [a + b for a, b in zip(base_m1, per_bank(("proj", "turn")))]

    def base_at(t):
        return [a + b * t for a, b in zip(base_0, per_bank(ALL))]

    def run(eng, body):
        body(Step(0, -2, ("turn",), [0] * NBANK))
        body(Step(0, -1, ("proj", "turn"), base_m1))
        with eng.Fori(0, loops) as i:
            body(Step(i, 0, ALL, base_at(0)))
            body(Step(i, 1, ALL, base_at(1)))
        t = n_blocks - 2
        body(Step(0, t, ("attn", "proj"), base_at(t)))
        body(Step(0, t + 1, ("attn",), [a + b for a, b in zip(base_at(t), per_bank(("attn", "proj")))]))

    def kv_before(st, c):
        par = st.off % 2
        per = 2 * TPB - 1
        return st.i * per + (st.off // 2 * per + TPB * par + c)

    def first_tile(st, c):
        return st.off % 2 == 0 and c == 0

    def last_tile(st, c):
        return st.off % 2 == 1 and c == TPB - 1

    def phi_index(kind, g):
        return 2 * g + (kind == "K")

    block = ctx.enter_context(nc.Block())

    @block.sync
    def _(sp):
        def load_x(st):
            a = st.off + 2
            for c in range(TPB):
                if a > 0:
                    wait_alone(sp, x_normed, st.lin(TPB, a - 1, c + 1))
                sp.dma_start(x_in[:, c, :], x_t[st.lin(TPB, a, c), :, :]).then_inc(x_load[c].handle, 16)

        def load_diag(st, off, c, h):
            wait(sp, scored, st.lin(TPB * KD, off, (c - 1) * KD + 2 * h + 2))
            wait(sp, lo_parts, st.lin(4 * TPB, off, 4 * c + 2 * h + 1))
            for j in range(HPG):
                rows = slice(HD * j, HD * (j + 1))
                sp.dma_start(q_diag.bitcast(F32)[rows, 2 * h:2 * h + 2, :, j, :],
                             q_hl.bitcast(F32)[rows, 2 * h:2 * h + 2]
                             ).then_inc(diag_load[h].handle, 16)

        def load_res(st, off, c):
            if not (off == 0 and c < 2 and isinstance(st.i, int)):
                wait(sp, stored[c % 2], st.lin(TPB // 2 * 16, off, c // 2 * 16))
                wait_alone(sp, x1_stat, st.lin(TPB, off, c - 1))
            sp.dma_start(res[:, c % 2, :], x_t[st.lin(TPB, off, c), :, :]
                         ).then_inc(res_load[c % 2].handle, 16)

        def body(st):
            t = st.off
            if not st.has("attn"):
                load_x(st)
                if st.has("proj"):
                    load_res(st, t + 1, 0)
                    for h in range(2):
                        load_diag(st, t + 1, 0, h)
                return
            for c in range(TPB):
                last = c == TPB - 1
                nxt = (t + 1, 0) if last else (t, c + 1)
                if c == 0 and st.has("turn"):
                    load_x(st)
                if not last or st.has("proj"):
                    load_res(st, *nxt)
                    for h in range(2):
                        load_diag(st, *nxt, h)
                k, n = st.use(("O", (c, 1)))
                wait_alone(sp, free[k], n + 1)
                sp.dma_start(out_t[st.lin(TPB, t, c), :, :], res[:, c % 2, :]
                             ).then_inc(stored[c % 2].handle, 16)

        give(sp, *stored)
        run(sp, body)
        for s in stored:
            wait(sp, s, n_blocks * TPB // 2 * 16)

    @block.tensor
    def _(pe):
        def turn(st, c):
            u = ("X", c)
            bank = claim(pe, st, u)
            wait(pe, x_normed, st.lin(TPB, st.off + 2, c + 1))
            for k in range(KD):
                mm = pe.transpose(bank[:, k * P:(k + 1) * P], x_norm[:, c % 2, k * P:(k + 1) * P], ident)
            filled(u, mm)

        def project(st, kind, g):
            u = (kind, g)
            w = w_q if kind == "Q" else w_k
            bank = claim(pe, st, u)
            n = 0
            for k in range(KD):
                for a, b in ((0, 0), (0, 1), (1, 0)):
                    mm = pe.matmul(bank, w[a][:, k, g * P:(g + 1) * P], xt[b][:, k, :],
                                   start=n == 0, stop=n == 3 * KD - 1)
                    n += 1
            filled(u, mm)

        def two_halves(st, kind, c, rows, w):
            banks = [claim(pe, st, (kind, (c, h))) for h in range(2)]
            n = 0
            for k in range(KD):
                for a, b in ((0, 0), (0, 1), (1, 0)):
                    for h in range(2):
                        mm = pe.matmul(banks[h][:, 0:HW], rows[a](k), w[b][:, k, h, :],
                                       start=n == 0, stop=n == 3 * KD - 1)
                        if n == 3 * KD - 1:
                            filled((kind, (c, h)), mm)
                    n += 1

        def chunk(st, c, m):
            for kind, j in CHUNKS[c, m]:
                if kind != "V":
                    project(st, kind, j)
                else:
                    two_halves(st, "V", j, [lambda k, h=h: xt[h][:, k, j * P:(j + 1) * P] for h in range(2)], w_v)

        def denominators(st):
            u = ("DEN", 0)
            bank = claim(pe, st, u)
            wait(pe, prod, st.lin(KD, st.off + 1, KD))
            for g in range(KD):
                mm = pe.matmul(bank[g * HD:(g + 1) * HD, :], head_cols, k_sum[:, g, :], start=True, stop=True,
                               tile_position=(0, g * HD))
            filled(u, mm)

        def spread_reciprocals(st, groups):
            if groups[0] == 0:
                wait(pe, rden_lo, st.lin(1, st.off + 1, 1))
            for g in groups:
                u = ("R", g)
                bank = claim(pe, st, u)
                for h in range(2):
                    mm = pe.matmul(bank, spread[:, g, :], rden[h], start=h == 0, stop=h == 1)
                filled(u, mm)

        def scores(st, c, g):
            idx = st.lin(TPB * KD, st.off, c * KD + g)
            wait(pe, masked, idx - 1)
            if g % 2 == 0:
                wait(pe, lo_parts, st.lin(4 * TPB, st.off, 4 * c + g + 2))
                wait(pe, diag_load[g // 2], st.lin(TPB * 16 * HPG, st.off, (c + 1) * 16 * HPG))
            for n, (a, b) in enumerate(((0, 0), (0, 1), (1, 0))):
                mm = pe.matmul(s_ps[:, g % 2], k_hl[:, g, a], q_diag[:, g, b], start=n == 0, stop=n == 2)
            done(scored, mm)

        def turn_keys(st, c):
            u = ("T", c)
            bank = claim(pe, st, u)
            for g in range(KD):
                mm = pe.transpose(bank[:, g * P:(g + 1) * P], k_t[:, st.off % 2, g, c * P:(c + 1) * P], ident)
            filled(u, mm)

        def from_state(st, c):
            wait(pe, o_lo, st.lin(TPB, st.off, c))
            if first_tile(st, c):
                return
            wait(pe, kv_masked, kv_before(st, c))
            for g in range(KD):
                pe.matmul(num_ps[:, g], kv_diag[:, g], q_div[:, g, c * P:(c + 1) * P],
                          start=g == 0, stop=False, skip_group_check=True)

        def from_tile(st, c, g):
            wait(pe, masked, st.lin(TPB * KD, st.off, c * KD + g + 1))
            for j in range(HPG):
                col = (g * HPG + j) * HD
                mm = pe.matmul(num_ps[j * HD:(j + 1) * HD, g], v_tok[:, c, col:col + HD],
                               s_mask[:, g % 2, j], start=first_tile(st, c) and g == 0,
                               stop=g == KD - 1, skip_group_check=True, tile_position=(0, j * HD))
            if g == KD - 1:
                done(summed, mm)

        def add_state(st, c):
            if last_tile(st, c):
                return
            wait_free(pe, st, ("T", c))
            for g in range(KD):
                mm = pe.matmul(kv_ps[:, g], k_tok[:, g * P:(g + 1) * P], v_tok[:, c, g * P:(g + 1) * P],
                               start=first_tile(st, c) and g == 0, stop=g == KD - 1, skip_group_check=True)
            done(kv_done, mm)

        def body(st):
            attn, proj, turns = (st.has(p) for p in ALL)
            if not attn and not proj:
                for c in range(TPB):
                    turn(st, c)
                return
            for c in range(TPB):
                last = c == TPB - 1
                if last and proj:
                    denominators(st)
                if attn:
                    scores(st, c, 0)
                    scores(st, c, 1)
                    turn_keys(st, c)
                if last and turns:
                    turn(st, 0)
                if proj:
                    if c == 0:
                        wait_step_before(pe, st, "X")
                    chunk(st, c, 0)
                if last and turns:
                    turn(st, 1)
                if attn:
                    if c == 0:
                        wait_step_before(pe, st, "V")
                    from_state(st, c)
                    from_tile(st, c, 0)
                    scores(st, c, 2)
                    from_tile(st, c, 1)
                    scores(st, c, 3)
                    add_state(st, c)
                if proj:
                    if last:
                        spread_reciprocals(st, (0, 1))
                    chunk(st, c, 1)
                if attn:
                    from_tile(st, c, 2)
                    from_tile(st, c, 3)
                if last and proj:
                    spread_reciprocals(st, (2, 3))
                if last and turns:
                    turn(st, 2)
                if proj:
                    chunk(st, c, 2)
                if last and turns:
                    turn(st, 3)
                if attn:
                    wait(pe, o_lo, st.lin(TPB, st.off, c + 1))
                    two_halves(st, "O", c, [lambda k, h=h: o_t[h][:, k, :] for h in range(2)], w_o)

        give(pe, scored)
        run(pe, body)

    @block.scalar
    def _(act):
        def relu_exp(st, kind, g):
            u, m = (kind, g), kind == "K"
            bank = wait_full(act, st, u)
            if g:
                wait_free(act, st, (kind, g - 1))
            else:
                wait_step_before(act, st, kind)
            n = st.lin(2 * KD, st.off + 1, phi_index(kind, g) + 1)
            done(phi_relu, act.activation(e_tmp[:, m], bank, ACT.Relu, bias=bias_n[:, m, g:g + 1], scale=-1.0))
            wait(act, phi_relu, n)
            done(phi_exp, act.activation(e_tmp[:, m], e_tmp[:, m], ACT.Exp, scale=-1.0))

        def turn_hi(st, c):
            bank = wait_full(act, st, ("X", c))
            done(xt_hi, act.activation(xt[0][:, :, c * P:(c + 1) * P], bank.rearrange("p (k t) -> p k t", k=KD),
                                       ACT.Copy))

        def chunk(st, c, m):
            for kind, j in CHUNKS[c, m]:
                if kind != "V":
                    relu_exp(st, kind, j)

        def high_parts(st, off, c, h):
            gs, t = slice(2 * h, 2 * h + 2), slice(c * P, (c + 1) * P)
            wait(act, diag_load[h], st.lin(TPB * 16 * HPG, off, c * 16 * HPG))
            if off > st.off:
                wait_free(act, st, ("R", 2 * h + 1))
            done(hi_parts, act.activation(q_hl[:, gs, 0], q_div[:, gs, t], ACT.Copy))
            wait(act, scored, st.lin(TPB * KD, off, (c - 1) * KD + 2 * h + 2))
            done(hi_parts, act.activation(k_hl[:, gs, 0], k_t[:, off % 2, gs, t], ACT.Copy))

        def next_high(st, c, h):
            if c < TPB - 1:
                if st.has("attn"):
                    high_parts(st, st.off, c + 1, h)
            elif st.has("proj"):
                high_parts(st, st.off + 1, 0, h)

        def body(st):
            attn, proj, turns = (st.has(p) for p in ALL)
            if not attn and not proj:
                for c in range(TPB):
                    turn_hi(st, c)
                return
            for c in range(TPB):
                last = c == TPB - 1
                if last and proj:
                    u = ("DEN", 0)
                    release(u, act.activation(den, wait_full(act, st, u), ACT.Copy, bias=DEN_EPS))
                if attn:
                    u = ("T", c)
                    release(u, act.activation(k_tok, wait_full(act, st, u), ACT.Copy))
                if last and turns:
                    turn_hi(st, 0)
                if proj:
                    chunk(st, c, 0)
                if last and turns:
                    turn_hi(st, 1)
                if last and proj:
                    wait(act, den_rec, st.lin(1, st.off + 1, 1))
                    done(rden_hi, act.activation(rden[0], den, ACT.Copy))
                next_high(st, c, 0)
                if proj:
                    chunk(st, c, 1)
                if attn:
                    wait(act, summed, st.lin(TPB, st.off, c + 1))
                    done(o_hi, act.activation(o_t[0], num_ps, ACT.Copy))
                if last and turns:
                    turn_hi(st, 2)
                next_high(st, c, 1)
                if proj:
                    chunk(st, c, 2)
                if last and turns:
                    turn_hi(st, 3)

        run(act, body)

    @block.vector
    def _(dve):
        def mask_scores(st, c, g):
            idx = st.lin(TPB * KD, st.off, c * KD + g)
            wait(dve, scored, idx + 1)
            done(masked, dve.tensor_tensor(s_mask[:, g % 2], s_ps[:, g % 2], repeat(causal, HPG), ALU.mult))

        def mask_state(st, c):
            if not last_tile(st, c):
                wait(dve, kv_done, kv_before(st, c) + 1)
                done(kv_masked, dve.tensor_tensor(kv_diag, kv_ps, repeat(diag_blocks, KD), ALU.mult))

        def phi(st, kind, g):
            u, m = (kind, g), kind == "K"
            bank = wait_full(dve, st, u)
            wait(dve, phi_exp, st.lin(2 * KD, st.off + 1, phi_index(kind, g) + 1))
            par = (st.off + 1) % 2
            out = k_t[:, par, g] if m else q_raw[:, g]
            release(u, dve.scalar_tensor_tensor(out, bank, bias[:, m, g:g + 1], e_tmp[:, m], ALU.add, ALU.max))

        def key_sums(st, g):
            par = (st.off + 1) % 2
            out = k_t[:, par, g]
            n = st.lin(KD, st.off + 1, g + 1)
            wait_free(dve, st, ("K", g))
            start = 0.0 if par == 0 else k_carry[:, g:g + 1]
            done(k_scan, dve.tensor_tensor_scan(k_sum[:, g], out, out, start, ALU.add, ALU.max))
            wait(dve, k_scan, n)
            done(k_carried, dve.tensor_copy(k_carry[:, g:g + 1], k_sum[:, g, BT - 1:BT]))

        def values(st, c):
            for h in range(2):
                u = ("V", (c, h))
                bank = wait_full(dve, st, u)
                dve.tensor_tensor(v_tok[:, c, h * DH:(h + 1) * DH], bank[:, 0:DH],
                                  bv_row[:, h * DH:(h + 1) * DH], ALU.add)
                release(u, dve.tensor_copy(gate_x[:, (st.off + 1) % 2, c, h * EH:(h + 1) * EH], bank[:, DH:HW]))

        def chunk(st, c, m):
            for kind, j in CHUNKS[c, m]:
                values(st, j) if kind == "V" else phi(st, kind, j)

        def chunk_sums(st, c, m):
            for kind, j in CHUNKS[c, m]:
                if kind == "K":
                    key_sums(st, j)

        def divide(st, groups):
            for g in groups:
                u = ("R", g)
                bank = wait_full(dve, st, u)
                release(u, dve.tensor_tensor(q_div[:, g], bank, q_raw[:, g], ALU.mult))

        def turn_lo(st, c):
            u = ("X", c)
            bank = wait_full(dve, st, u).rearrange("p (k t) -> p k t", k=KD)
            wait(dve, xt_hi, st.lin(TPB, st.off + 2, c + 1))
            t = slice(c * P, (c + 1) * P)
            release(u, dve.tensor_tensor(xt[1][:, :, t], bank, xt[0].bitcast(F32)[:, :, t], ALU.subtract))

        def moments(st, tiles):
            a = st.off + 2
            for c in tiles:
                wait(dve, x_load[c], st.lin(16, a, 16))
                done(x_stat, dve.bn_stats(stats[:, c], x_in[:, c]))
            if tiles[0] == 0:
                wait(dve, gx_done, st.lin(1, a - 1))
            for c in tiles:
                wait_alone(dve, x_stat, st.lin(TPB, a, c + 1))
                done(x_aggr, dve.bn_aggr(mv0[:, a % 2, c], stats[:, c]))

        def normalise(st, c):
            a = st.off + 2
            if c == 0:
                wait(dve, x_rstd, st.lin(1, a, 1))
            done(x_normed, dve.tensor_scalar(x_norm[:, c % 2], x_in[:, c], mv0[:, a % 2, c, 0:1],
                                             rstd0[:, a % 2, c:c + 1], ALU.subtract, ALU.mult))

        def residual(st, c):
            if c == 0:
                wait(dve, z_done, st.lin(1, st.off))
            wait(dve, res_bias, st.lin(TPB, st.off, c + 1))
            for h in range(2):
                u = ("O", (c, h))
                bank = wait_full(dve, st, u)
                cols = slice(h * DH, (h + 1) * DH)
                dve.tensor_tensor(res[:, c % 2, cols], bank[:, 0:DH], res[:, c % 2, cols], ALU.add)
                release(u, dve.tensor_tensor(gate_o[:, c, h * EH:(h + 1) * EH], bank[:, DH:HW],
                                             g_bo[:, h * EH:(h + 1) * EH], ALU.add))
            wait_free(dve, st, ("O", (c, 1)))
            done(x1_stat, dve.bn_stats(stats1[:, c], res[:, c % 2]))
            wait_alone(dve, x1_stat, st.lin(TPB, st.off, c + 1))
            done(x1_aggr, dve.bn_aggr(mv1[:, c], stats1[:, c]))

        def body(st):
            attn, proj, turns = (st.has(p) for p in ALL)
            if not attn:
                moments(st, range(TPB))
            if not attn and not proj:
                for c in range(2):
                    normalise(st, c)
                for c in range(TPB):
                    turn_lo(st, c)
                    if c < 2:
                        normalise(st, c + 2)
                return
            for c in range(TPB):
                last = c == TPB - 1
                if attn:
                    mask_scores(st, c, 0)
                    mask_scores(st, c, 1)
                if last and proj:
                    wait_free(dve, st, ("DEN", 0))
                    done(den_rec, dve.reciprocal(den, den))
                if last and turns:
                    turn_lo(st, 0)
                    normalise(st, 2)
                if proj:
                    chunk(st, c, 0)
                    chunk_sums(st, c, 0)
                if last and turns:
                    turn_lo(st, 1)
                    normalise(st, 3)
                if attn:
                    mask_scores(st, c, 2)
                    mask_scores(st, c, 3)
                    mask_state(st, c)
                    if c == 1 and turns:
                        moments(st, (0, 1))
                if last and proj:
                    divide(st, (0, 1))
                if proj:
                    chunk(st, c, 1)
                if last and proj:
                    divide(st, (2, 3))
                if attn:
                    wait(dve, o_hi, st.lin(TPB, st.off, c + 1))
                    done(o_lo, dve.tensor_tensor(o_t[1], num_ps, o_t[0].bitcast(F32), ALU.subtract))
                if last and turns:
                    turn_lo(st, 2)
                if proj:
                    chunk_sums(st, c, 1)
                if attn:
                    if c == 1 and turns:
                        moments(st, (2, 3))
                if proj:
                    chunk(st, c, 2)
                    chunk_sums(st, c, 2)
                if c == 2 and turns:
                    normalise(st, 0)
                    normalise(st, 1)
                if last and turns:
                    turn_lo(st, 3)
                if attn:
                    residual(st, c)

        give(dve, *free, masked, o_lo, x1_stat)
        run(dve, body)

    @block.gpsimd
    def _(pool):
        def rstds(st):
            a = st.off + 2
            wait_alone(pool, x_aggr, st.lin(TPB, a, TPB))
            done(x_var, pool.tensor_scalar(var0[:, a % 2], mv0[:, a % 2, :, 1], LN_EPS, None, ALU.add))
            wait(pool, x_var, st.lin(1, a, 1))
            done(x_rstd, pool.tensor_tensor(rstd0[:, a % 2], var0[:, a % 2], neg_half, ALU.pow))

        def products(st, g):
            wait(pool, k_carried, st.lin(KD, st.off + 1, g + 1))
            done(prod, pool.tensor_tensor(k_sum[:, g], k_sum[:, g], q_raw[:, g], ALU.mult))

        def linked(s, st, off, per):
            n = [0]

            def link(ins):
                n[0] += 1
                done(s, ins)
                wait(pool, s, st.lin(per, off, n[0]))
            return link

        def gate_in(st):
            b = (st.off + 1) % 2
            link = linked(gx_link, st, st.off + 1, 3)
            wait_free(pool, st, ("V", (TPB - 1, 1)))
            wait_free(pool, st, ("V", (TPB - 1, 0)))
            link(pool.tensor_tensor(std0, var0[:, b], rstd0[:, b], ALU.mult))
            link(pool.tensor_tensor(gate_x[:, b], gate_x[:, b], over(std0, E), ALU.mult))
            link(pool.tensor_tensor(z_a, repeat(g_sum, TPB), over(mv0[:, b, :, 0:1], E), ALU.mult))
            done(gx_done, pool.tensor_tensor(gate_x[:, b], gate_x[:, b], z_a, ALU.add))

        def logits(st):
            b = st.off % 2
            link = linked(z_link, st, st.off, 6)
            wait_free(pool, st, ("O", (TPB - 1, 1)))
            wait(pool, x1_aggr, st.lin(TPB, st.off, TPB))
            wait_alone(pool, gx_done, st.lin(1, st.off, 1))
            link(pool.tensor_scalar(var1, mv1[:, :, 1], LN_EPS, None, ALU.add))
            link(pool.tensor_tensor(rstd1, var1, neg_half, ALU.pow))
            link(pool.tensor_tensor(z_b, repeat(g_sum, TPB), over(mv1[:, :, 0:1], E), ALU.mult))
            link(pool.tensor_tensor(z_b, gate_x[:, b], z_b, ALU.subtract))
            link(pool.tensor_tensor(z_b, z_b, gate_o, ALU.add))
            tiles = st.lin(TPB, st.off)
            link(pool.tensor_tensor(z_all[:, bass.ds(tiles, TPB), :], z_b, over(rstd1, E), ALU.mult))
            done(z_done, pool.tensor_copy(keepers["moments"][:, bass.ds(tiles, TPB), 0:1], mv1[:, :, 0:1]))
            pool.tensor_copy(keepers["moments"][:, bass.ds(tiles, TPB), 1:2], rstd1.unsqueeze(2))

        def chunk(st, c, m):
            for kind, j in CHUNKS[c, m]:
                if kind == "K":
                    products(st, j)

        def low_parts(st, off, c, h):
            gs, t = slice(2 * h, 2 * h + 2), slice(c * P, (c + 1) * P)
            for n, (parts, whole) in enumerate(((q_hl, q_div[:, gs, t]), (k_hl, k_t[:, off % 2, gs, t]))):
                wait(pool, hi_parts, st.lin(4 * TPB, off, 4 * c + 2 * h + n + 1))
                done(lo_parts, pool.tensor_tensor(parts[:, gs, 1], whole, parts.bitcast(F32)[:, gs, 0],
                                                  ALU.subtract))

        def next_low(st, c, h):
            if c < TPB - 1:
                if st.has("attn"):
                    low_parts(st, st.off, c + 1, h)
            elif st.has("proj"):
                low_parts(st, st.off + 1, 0, h)

        def body(st):
            attn, proj, turns = (st.has(p) for p in ALL)
            if not attn and not proj:
                rstds(st)
                return
            for c in range(TPB):
                last = c == TPB - 1
                if attn:
                    wait(pool, res_load[c % 2], st.lin(TPB // 2 * 16, st.off, (c // 2 + 1) * 16))
                    done(res_bias, pool.tensor_tensor(res[:, c % 2], res[:, c % 2], bo_row, ALU.add))
                if proj:
                    chunk(st, c, 0)
                if last and proj:
                    wait(pool, rden_hi, st.lin(1, st.off + 1, 1))
                    done(rden_lo, pool.tensor_tensor(rden[1], den, rden[0].bitcast(F32), ALU.subtract))
                next_low(st, c, 0)
                if c == 1 and turns:
                    rstds(st)
                if proj:
                    chunk(st, c, 1)
                next_low(st, c, 1)
                if proj:
                    chunk(st, c, 2)
                if last and proj:
                    gate_in(st)
                if last and attn:
                    logits(st)

        give(pool, z_done)
        run(pool, body)


def choose(nc, io, keepers, capacity):
    z, keep, any_kept, ones = (keepers[n] for n in ("z_all", "keep", "any_kept", "ones"))
    T = z.shape[1]
    with ExitStack() as ctx:
        def sb(name, shape, dt=F32):
            return ctx.enter_context(nc.sbuf_tensor(name, shape, dt))[:]

        eq, key, left, picked = (sb(n, [P, T, E]) for n in ("eq", "key", "left", "picked"))
        top = sb("top", [P, T])
        order = sb("order", [P, E])
        count = sb("count", [P, E])
        total = ctx.enter_context(nc.psum_tensor("total", [P, 512], F32))[:]
        dve_done, act_done, pe_done = (ctx.enter_context(nc.semaphore(n))
                                       for n in ("choose_dve", "choose_act", "choose_pe"))
        EXP_READY = E + 2
        wide = lambda ap: ap.unsqueeze(2).to_broadcast([P, T, E])
        block = ctx.enter_context(nc.Block())
        counted = []

        @block.vector
        def _(dve):
            n = [0]

            def link(ins):
                n[0] += 1
                ins.then_inc(dve_done, 1)
                dve.wait_ge(dve_done, n[0])

            def pick(values, out):
                link(dve.tensor_reduce(top, values, AXX, ALU.max))
                link(dve.tensor_tensor(eq, values, wide(top), ALU.is_equal))
                link(dve.tensor_tensor(key, eq, order.unsqueeze(1).to_broadcast([P, T, E]), ALU.mult))
                link(dve.tensor_reduce(top, key, AXX, ALU.max))
                link(dve.tensor_tensor(out, key, wide(top), ALU.is_equal))

            for e in range(E):
                link(dve.memset(order[:, e:e + 1], float(E - e)))
            link(dve.tensor_reduce(top, z, AXX, ALU.max))
            link(dve.tensor_tensor(z, z, wide(top), ALU.subtract))
            assert n[0] == EXP_READY
            dve.wait_ge(act_done, 1)
            link(dve.tensor_reduce(top, z, AXX, ALU.add))
            link(dve.reciprocal(top, top))
            link(dve.tensor_tensor(z, z, wide(top), ALU.mult))
            pick(z, picked)
            link(dve.scalar_tensor_tensor(left.rearrange("p t e -> p (t e)"), picked.rearrange("p t e -> p (t e)"),
                                          -2.0, z.rearrange("p t e -> p (t e)"), ALU.mult, ALU.add))
            pick(left, eq)
            link(dve.tensor_tensor(picked, picked, eq, ALU.add))
            link(dve.tensor_tensor(z, z, picked, ALU.mult))
            link(dve.tensor_reduce(count, picked.rearrange("p t e -> p e t"), AXX, ALU.add))
            counted.append(n[0])
            dve.wait_ge(pe_done, 1)
            link(dve.tensor_scalar(keep, total[:, 0:E], float(capacity), None, ALU.is_le))
            link(dve.tensor_reduce(any_kept, keep, AXX, ALU.max))

        @block.scalar
        def _(act):
            act.wait_ge(dve_done, EXP_READY)
            act.activation(z, z, ACT.Exp).then_inc(act_done, 1)

        @block.tensor
        def _(pe):
            pe.wait_ge(dve_done, counted[0])
            pe.matmul(total[:, 0:E], ones, count, start=True, stop=True).then_inc(pe_done, 1)
    nc.all_engine_barrier()


def experts(nc, io, n_blocks, keepers):
    wts, keep, any_kept, moments, ident = (keepers[n] for n in ("z_all", "keep", "any_kept", "moments", "ident"))
    out_b = io["out"].rearrange("(n c p) d -> n p c d", c=TPB, p=P)
    with ExitStack() as ctx:
        def sb(name, shape, dt=F32):
            return ctx.enter_context(nc.sbuf_tensor(name, shape, dt))[:]

        def sem(name, credit=0):
            return Sem(ctx.enter_context(nc.semaphore(name)), credit)

        w1 = sb("e_w1", [P, 2, KD, D])
        w2 = sb("e_w2", [P, 2, KD, D])
        b1 = sb("e_b1", [P, 2, KD])
        b2 = sb("e_b2", [P, 2, D])
        acc = sb("e_acc", [P, TPB, D])
        norm = sb("e_norm", [P, TPB, D])
        mom = sb("e_mom", [P, TPB, 2])
        wt = sb("e_wt", [P, TPB, E])
        xt = sb("e_xt", [P, KD, BT])
        hid = sb("e_hid", [P, KD, BT])
        y_b = sb("e_y", [P, D])
        pt = ctx.enter_context(nc.psum_tensor("e_pt", [P, TPB, 512], F32))[:]
        ph = ctx.enter_context(nc.psum_tensor("e_ph", [P, 2, 512], F32))[:]
        py = ctx.enter_context(nc.psum_tensor("e_py", [P, 2, 512], F32))[:]

        x1_load, w_load = sem("e_x1_load"), [sem(f"e_w_load{n}") for n in range(2)]
        copied, normed, turned, turned_out = sem("e_copied"), sem("e_normed"), sem("e_turned"), sem("e_turned_out", CREDIT)
        h_full, h_out = sem("e_h_full"), sem("e_h_out", CREDIT)
        y_full, y_bias, y_added = sem("e_y_full"), sem("e_y_bias"), sem("e_y_added", 2 * TPB)
        out_store, passed = sem("e_out_store", 16), {e.engine: sem(f"e_passed{n}") for n, e in
                                                     enumerate((nc.sync, nc.vector))}

        def wait(eng, s, n):
            eng.wait_ge(s.handle, n + s.credit)
            if eng.engine in passed:
                eng.sem_inc(passed[eng.engine].handle, 1)

        def done(s, ins):
            ins.then_inc(s.handle, 1)

        def give(eng, *sems):
            for s in sems:
                eng.sem_inc(s.handle, s.credit)

        def over_experts(eng, i, body):
            with eng.Fori(0, E // 2) as j:
                for n in range(2):
                    body(n, i * (E // 2) + j + 1, j * 2 + n, i * E + j * 2 + n)

        block = ctx.enter_context(nc.Block())

        def where_kept(eng, body):
            flag = eng.value_load(any_kept[0:1, 0:1], min_val=0, max_val=1)
            with eng.If(flag > 0):
                with eng.Fori(0, n_blocks) as i:
                    body(i)

        @block.sync
        def _(sp):
            def body(i):
                wait(sp, out_store, i * 16)
                sp.dma_start(acc, out_b[i, :, :, :]).then_inc(x1_load.handle, 16)

                def load(n, uses, e, idx):
                    wait(sp, y_added, (idx - 1) * TPB)
                    for dst, src in ((w1[:, n], io["w1_t"]), (w2[:, n], io["w2_t"])):
                        sp.dma_start(dst, src[e, :, :].rearrange("(k p) d -> p k d", p=P)
                                     ).then_inc(w_load[n].handle, 16)
                    with nc.allow_non_contiguous_dma("a column of biases"):
                        sp.dma_start(b1[:, n], io["b1"][e, :].rearrange("(k p) -> p k", p=P)
                                     ).then_inc(w_load[n].handle, 16)
                    sp.dma_start(b2[:, n], io["b2"][bass.ds(e, 1), :].to_broadcast([P, D])
                                 ).then_inc(w_load[n].handle, 16)
                over_experts(sp, i, load)
                wait(sp, y_added, (i + 1) * (E * TPB))
                sp.dma_start(out_b[i, :, :, :], acc).then_inc(out_store.handle, 16)

            give(sp, out_store)
            where_kept(sp, body)
            flag = sp.value_load(any_kept[0:1, 0:1], min_val=0, max_val=1)
            with sp.If(flag > 0):
                sp.wait_ge(out_store.handle, (n_blocks + 1) * 16)

        @block.vector
        def _(dve):
            def body(i):
                tiles = bass.ds(i * TPB, TPB)
                wait(dve, x1_load, (i + 1) * 16)
                done(copied, dve.tensor_copy(mom, moments[:, tiles, :]))
                done(copied, dve.tensor_tensor(wt, wts[:, tiles, :], keep.unsqueeze(1).to_broadcast([P, TPB, E]),
                                               ALU.mult))
                wait(dve, copied, (i + 1) * 2)
                for c in range(TPB):
                    done(normed, dve.tensor_scalar(norm[:, c], acc[:, c], mom[:, c, 0:1], mom[:, c, 1:2],
                                                   ALU.subtract, ALU.mult))

                def add(n, uses, e, idx):
                    for c in range(TPB):
                        m = idx * TPB + c
                        wait(dve, y_full, m + 1)
                        wait(dve, y_added, m)
                        done(y_bias, dve.tensor_tensor(y_b, py[:, c % 2], b2[:, n], ALU.add))
                        wait(dve, y_bias, m + 1)
                        done(y_added, dve.scalar_tensor_tensor(acc[:, c], y_b, wt[:, c, bass.ds(e, 1)], acc[:, c],
                                                               ALU.mult, ALU.add))
                over_experts(dve, i, add)

            give(dve, y_added)
            where_kept(dve, body)

        @block.tensor
        def _(pe):
            def body(i):
                for c in range(TPB):
                    wait(pe, normed, i * TPB + c + 1)
                    if c == 0:
                        wait(pe, turned_out, i * TPB)
                    for k in range(KD):
                        mm = pe.transpose(pt[:, c, k * P:(k + 1) * P], norm[:, c, k * P:(k + 1) * P], ident)
                    done(turned, mm)

                def expert(n, uses, e, idx):
                    for g in range(KD):
                        wait(pe, h_out, idx * KD + g - 1)
                        if g == 0:
                            wait(pe, w_load[n], uses * 64)
                            wait(pe, turned_out, (i + 1) * TPB)
                        for k in range(KD):
                            mm = pe.matmul(ph[:, g % 2], w1[:, n, k, g * P:(g + 1) * P], xt[:, k],
                                           start=k == 0, stop=k == KD - 1)
                        done(h_full, mm)
                    wait(pe, h_out, (idx + 1) * KD)
                    for c in range(TPB):
                        wait(pe, y_added, idx * TPB + c - 1)
                        for g in range(KD):
                            mm = pe.matmul(py[:, c % 2], hid[:, g, c * P:(c + 1) * P], w2[:, n, g],
                                           start=g == 0, stop=g == KD - 1)
                        done(y_full, mm)
                over_experts(pe, i, expert)

            where_kept(pe, body)

        @block.scalar
        def _(act):
            def body(i):
                for c in range(TPB):
                    wait(act, turned, i * TPB + c + 1)
                    done(turned_out, act.activation(xt[:, :, c * P:(c + 1) * P],
                                                    pt[:, c].rearrange("p (k t) -> p k t", k=KD), ACT.Copy))

                def hidden(n, uses, e, idx):
                    for g in range(KD):
                        wait(act, h_full, idx * KD + g + 1)
                        done(h_out, act.activation(hid[:, g], ph[:, g % 2], ACT.Silu, bias=b1[:, n, g:g + 1]))
                over_experts(act, i, hidden)

            give(act, turned_out, h_out)
            where_kept(act, body)


def program(nc, io, n_tok):
    n_tiles = n_tok // P
    with ExitStack() as keep:
        def sb(name, shape, dt=F32):
            return keep.enter_context(nc.sbuf_tensor(name, shape, dt))[:]

        keepers = {"z_all": sb("z_all", [P, n_tiles, E]), "moments": sb("moments", [P, n_tiles, 2]),
                   "ident": sb("ident", [P, P]), "ones": sb("ones", [P, P]),
                   "keep": sb("keep", [P, E]), "any_kept": sb("any_kept", [P, 1], I32)}
        with ExitStack() as ctx:
            attention(nc, ctx, io, n_tok // BT, keepers)
        nc.all_engine_barrier()
        choose(nc, io, keepers, int(CAPACITY_FACTOR * n_tok / E))
        experts(nc, io, n_tok // BT, keepers)


def kernel(L0_attn_x, L0_attn_Wq, L0_attn_bq, L0_attn_Wk, L0_attn_bk, L0_attn_Wv, L0_attn_bv, L0_attn_Wo,
           L0_attn_bo, L0_ffn_gate_w, L0_ffn_w1, L0_ffn_b1, L0_ffn_w2, L0_ffn_b2):
    import concourse.bacc as bacc
    from concourse.bass_utils import run_bass_kernel_spmd

    x = np.asarray(L0_attn_x)
    n_tok = x.shape[0] * x.shape[1]
    arrays = {"x": x.reshape(n_tok, D), "wq_t": np.asarray(L0_attn_Wq).T, "wk_t": np.asarray(L0_attn_Wk).T,
              "wv_t": np.asarray(L0_attn_Wv).T, "wo_t": np.asarray(L0_attn_Wo).T, "wo": np.asarray(L0_attn_Wo),
              "bq": L0_attn_bq, "bk": L0_attn_bk, "bv": L0_attn_bv, "bo": L0_attn_bo,
              "gate": np.asarray(L0_ffn_gate_w).T,
              "w1_t": np.asarray(L0_ffn_w1).transpose(0, 2, 1), "b1": L0_ffn_b1,
              "w2_t": np.asarray(L0_ffn_w2).transpose(0, 2, 1), "b2": L0_ffn_b2}
    arrays = {f"in_{name}": np.ascontiguousarray(a) for name, a in arrays.items()}

    nc = bacc.Bacc("TRN2", target_bir_lowering=False, num_devices=1)
    io = {name[3:]: nc.dram_tensor(name, a.shape, mybir.dt.from_np(a.dtype), kind="ExternalInput").ap()
          for name, a in arrays.items()}
    io["out"] = nc.dram_tensor("out", (n_tok, D), F32, kind="ExternalOutput").ap()
    program(nc, io, n_tok)
    results = run_bass_kernel_spmd(nc, [arrays], core_ids=[0])
    return results.results[0]["out"].reshape(x.shape)
```

```python
from contextlib import ExitStack

import numpy as np

import concourse.bass as bass
import concourse.mybir as mybir

F32 = mybir.dt.float32
F32R = mybir.dt.float32r
I32 = mybir.dt.int32
ALU = mybir.AluOpType
ACT = mybir.ActivationFunctionType
AXX = mybir.AxisListType.X

P = 128
HEADS, HD = 16, 32
D = HEADS * HD
KD = D // P
HPG = P // HD
TPB = 4
BT = TPB * P
E = 8
EH = E // 2
DH = D // 2
HW = DH + EH
LN_EPS = 1e-5
DEN_EPS = 1e-6
CAPACITY_FACTOR = 1.25
CREDIT = 2
NBANK = 4

CHUNKS = {(0, 0): [("Q", 0)], (0, 1): [("K", 0)], (0, 2): [("Q", 1)],
          (1, 0): [("K", 1)], (1, 1): [("Q", 2)], (1, 2): [("K", 2)],
          (2, 0): [("Q", 3)], (2, 1): [("K", 3)], (2, 2): [("V", 0)],
          (3, 0): [("V", 1)], (3, 1): [("V", 2)], (3, 2): [("V", 3)]}


def ring_uses():
    uses = []
    for c in range(TPB):
        last = c == TPB - 1
        uses += [("DEN", 0)] * last + [("T", c)] + [("X", 0)] * last
        for n in range(3):
            if last and n == 1:
                uses += [("R", 0), ("R", 1)]
            for kind, j in CHUNKS[c, n]:
                uses += [(kind, j)] if kind != "V" else [("V", (j, 0)), ("V", (j, 1))]
            if last and n == 1:
                uses += [("R", 2), ("R", 3), ("X", 2)]
            elif last:
                uses += [("X", n + 1)]
        uses += [("O", (c, 0)), ("O", (c, 1))]
    return uses


USES = ring_uses()
BANK = {u: (n - (n > USES.index(("X", 1)))) % NBANK for n, u in enumerate(USES)}
assert (len(USES) - 1) % NBANK == 0


def part_of(kind):
    return "attn" if kind in ("T", "O") else "turn" if kind == "X" else "proj"


def uses_of(parts):
    return [u for u in USES if part_of(u[0]) in parts]


def per_bank(parts):
    return [sum(BANK[u] == k for u in uses_of(parts)) for k in range(NBANK)]


ALL = ("attn", "proj", "turn")


class Step:

    def __init__(self, i, off, parts, base):
        self.i, self.off, self.parts, self.base = i, off, parts, base

    def has(self, part):
        return part in self.parts

    def lin(self, k, off, c=0):
        return self.i * (2 * k) + (k * off + c)

    def before(self, k):
        return self.base[k] if isinstance(self.i, int) else self.i * (2 * per_bank(ALL)[k]) + self.base[k]

    def use(self, u):
        k = BANK[u]
        rank = sum(BANK[v] == k for v in uses_of(self.parts)[:uses_of(self.parts).index(u)])
        n = self.base[k] + rank
        if isinstance(self.i, int):
            return k, n
        return k, self.i * (2 * per_bank(ALL)[k]) + n



class Sem:

    def __init__(self, handle, credit=0):
        self.handle, self.credit = handle, credit


def choosing(dve, z, order, count, shape, scratch, done, before, exp_wait):
    eq, key, left, picked, top = scratch
    n = [before]

    def link(ins):
        n[0] += 1
        ins.then_inc(done.handle, 1)
        dve.wait_ge(done.handle, n[0])

    top_wide = top.unsqueeze(2).to_broadcast(shape)
    order_wide = order.unsqueeze(1).to_broadcast(shape)

    def pick(values, out):
        return [lambda: dve.tensor_reduce(top, values, AXX, ALU.max),
                lambda: dve.tensor_tensor(eq, values, top_wide, ALU.is_equal),
                lambda: dve.tensor_tensor(key, eq, order_wide, ALU.mult),
                lambda: dve.tensor_reduce(top, key, AXX, ALU.max),
                lambda: dve.tensor_tensor(out, key, top_wide, ALU.is_equal)]

    def sums():
        exp_wait()
        return dve.tensor_reduce(top, z, AXX, ALU.add)

    steps = [lambda: dve.tensor_reduce(top, z, AXX, ALU.max),
             lambda: dve.tensor_tensor(z, z, top_wide, ALU.subtract),
             sums,
             lambda: dve.reciprocal(top, top),
             lambda: dve.tensor_tensor(z, z, top_wide, ALU.mult),
             *pick(z, picked),
             lambda: dve.tensor_scalar(left, picked, -2.0, None, ALU.mult),
             lambda: dve.tensor_tensor(left, left, z, ALU.add),
             *pick(left, eq),
             lambda: dve.tensor_tensor(picked, picked, eq, ALU.add),
             lambda: dve.tensor_tensor(z, z, picked, ALU.mult),
             lambda: dve.tensor_reduce(count, picked.rearrange("p t e -> p e t"), AXX, ALU.add)]
    assert len(steps) == CHOOSE_STEPS
    return [lambda s=s: link(s()) for s in steps]


CHOOSE_STEPS, SHIFTED = 20, 2


def attention(nc, ctx, io, n_blocks, keepers, capacity):
    z_all, ident, ones, keep, any_kept = (keepers[n] for n in ("z_all", "ident", "ones", "keep", "any_kept"))
    x_t = io["x"].rearrange("(n p) d -> n p d", p=P)
    out_t = io["out"].rearrange("(n p) d -> n p d", p=P)

    def sb(name, shape, dt=F32):
        return ctx.enter_context(nc.sbuf_tensor(name, shape, dt))[:]

    def ps(name, shape):
        return ctx.enter_context(nc.psum_tensor(name, shape, F32))[:]

    def sem(name, credit=0):
        return Sem(ctx.enter_context(nc.semaphore(name)), credit)

    w_q = [sb(f"wq_{h}", [P, KD, D], F32R) for h in ("hi", "lo")]
    w_k = [sb(f"wk_{h}", [P, KD, D], F32R) for h in ("hi", "lo")]
    w_v = [sb(f"wv_{h}", [P, KD, 2, HW], F32R) for h in ("hi", "lo")]
    w_o = [sb(f"wo_{h}", [P, KD, 2, HW], F32R) for h in ("hi", "lo")]
    x_in = sb("x_in", [P, TPB, D])
    xt = [sb(f"xt_{h}", [P, KD, BT], F32R) for h in ("hi", "lo")]
    q_raw = sb("q_raw", [P, KD, BT])
    q_div = sb("q_div", [P, KD, BT])
    k_high = sb("k_high", [P, KD, P], F32R)
    k_low = sb("k_low", [P, KD, P], F32R)
    k_more = sb("k_more", [P, KD, 2, P], F32R)
    q_high = sb("q_high", [P, KD, HPG, P], F32R)
    q_more = sb("q_more", [P, KD, 2, 2, P], F32R)
    k_t = sb("k_t", [P, 2, KD, BT])
    k_sum = sb("k_sum", [P, KD, BT])
    k_carry = sb("k_carry", [P, KD])
    e_tmp = sb("e_tmp", [P, 2, BT])
    v_tok = sb("v_tok", [P, TPB, D])
    k_tok = sb("k_tok", [P, D])
    s_mask = sb("s_mask", [P, 2, HPG, P])
    kv_diag = sb("kv_diag", [P, KD, P])
    o_t = [sb(f"o_{h}", [P, KD, P], F32R) for h in ("hi", "lo")]
    res = sb("res", [P, 2, D])
    den = sb("den", [P, BT // 2])
    rden_high = sb("rden_high", [P, BT // 2], F32R)
    rden = sb("rden", [P, BT // 2], F32R)
    lo_rows = sb("lo_rows", [P, 1])
    causal = sb("causal", [P, P])
    diag_blocks = sb("diag_blocks", [P, P])
    head_cols = sb("head_cols", [P, 2, HD])
    spread = sb("spread", [P, 2, KD, P], F32R)
    bias = sb("bias", [P, 2, KD])
    bias_n = sb("bias_n", [P, 2, KD])
    bv_row = sb("bv_row", [P, D])
    bo_row = sb("bo_row", [P, D])
    bo_col = sb("bo_col", [P, KD])
    gw = sb("gw", [P, KD, E])
    gw_bo = sb("gw_bo", [P, KD, E])
    g_sum = sb("g_sum", [P, E])
    g_bo = sb("g_bo", [P, E])
    stats = sb("stats", [P, TPB, 6])
    mv0 = sb("mv0", [P, 2, TPB, 2])
    var0 = sb("var0", [P, 2, TPB])
    rstd0 = sb("rstd0", [P, 2, TPB])
    std0 = sb("std0", [P, TPB])
    stats1 = sb("stats1", [P, TPB, 6])
    mv1 = sb("mv1", [P, TPB, 2])
    var1 = sb("var1", [P, TPB])
    rstd1 = sb("rstd1", [P, TPB])
    gate_x = sb("gate_x", [P, 2, TPB, E])
    gate_o = sb("gate_o", [P, TPB, E])
    order = sb("order", [P, E])
    count = sb("count", [P, 2, E])
    z_a = sb("z_a", [P, TPB, E])
    z_b = sb("z_b", [P, TPB, E])
    neg_half = sb("neg_half", [P, TPB])

    ring = ps("ring", [P, NBANK, 512])
    s_ps = ps("s_ps", [P, 2, HPG, P])
    num_ps = ps("num_ps", [P, KD, P])
    kv_ps = ps("kv_ps", [P, KD, P])

    def over(ap, n):
        ap = ap if len(ap.shape) == 3 else ap.unsqueeze(2)
        return ap.to_broadcast([ap.shape[0], ap.shape[1], n])

    def repeat(ap, n):
        return ap.unsqueeze(1).to_broadcast([ap.shape[0], n, ap.shape[1]])

    stages = {"wq_t": q_raw, "wk_t": k_t[:, 0], "wv_t": v_tok, "wo_t": k_t[:, 1], "wo": q_div}
    split_of = {"wq_t": w_q, "wk_t": w_k, "wv_t": w_v, "wo_t": w_o}
    SPLITS = list(split_of)
    spread_f = s_mask
    low = kv_diag[:, 0, 0:2 * KD * HPG].rearrange("p (s g j) -> p s g j", s=2, g=KD)
    w_load = {name: sem(f"load_{name}") for name in stages}
    ready = {name: sem(f"ready_{name}") for name in SPLITS}
    col_load, row_load, ident_set, const_set = (sem("col_load"), sem("row_load"), sem("ident_set"),
                                                sem("const_set"))
    bias_set, high_split, gate_sums, gate_split = (sem("bias_set"), sem("high_split"), sem("gate_sums"),
                                                   sem("gate_split"))
    COLS, ROWS, BIASES, CONSTS = 4 * 16, 2 * 16, 3, 21 + E
    READY = {"wq_t": 1, "wk_t": 1, "wv_t": 2, "wo_t": 4}

    def halves(ap):
        return ap.rearrange("p k h w -> p (k h) w")[:, :, 0:DH]

    def gates_of(ap):
        return ap.rearrange("p k h w -> p (k h) w")[:, :, DH:HW]

    def weights(name):
        stage, w = stages[name], split_of[name]
        if name in ("wq_t", "wk_t"):
            return stage, w
        return stage.rearrange("p k (h d) -> p (k h) d", h=2), [halves(w[0]), halves(w[1])]

    def load_weights(sp):
        for name, stage in stages.items():
            sp.dma_start(stage, io[name].rearrange("(k p) d -> p k d", p=P)).then_inc(w_load[name].handle, 16)

    def load_biases(act):
        with nc.allow_non_contiguous_dma("a few columns of biases"):
            for dst, src in ((bias[:, 0], io["bq"]), (bias[:, 1], io["bk"]), (bo_col, io["bo"])):
                act.dma_start(dst, src.rearrange("(k p) -> p k", p=P)).then_inc(col_load.handle, 16)
            act.dma_start(gw, io["gate"].rearrange("(k p) e -> p k e", p=P)).then_inc(col_load.handle, 16)
        for dst, src in ((bv_row, io["bv"]), (bo_row, io["bo"])):
            act.dma_start(dst, src.rearrange("(a d) -> a d", a=1).to_broadcast([P, D])
                          ).then_inc(row_load.handle, 16)

    def split_high(act, name):
        act.wait_ge(w_load[name].handle, 16)
        stage, parts = weights(name)
        act.activation(parts[0], stage, ACT.Copy).then_inc(high_split.handle, 1)

    def split_low(dve, name):
        dve.wait_ge(high_split.handle, SPLITS.index(name) + 1)
        stage, parts = weights(name)
        dve.tensor_tensor(parts[1], stage, parts[0].bitcast(F32), ALU.subtract).then_inc(ready[name].handle, 1)

    def split_gates(dve, name, gates, n):
        w = split_of[name]
        dve.tensor_copy(gates_of(w[0]), gates).then_inc(gate_split.handle, 1)
        dve.wait_ge(gate_split.handle, n + 1)
        dve.tensor_tensor(gates_of(w[1]), gates, gates_of(w[0].bitcast(F32)), ALU.subtract
                          ).then_inc(ready[name].handle, 1)

    def set_biases(dve):
        dve.wait_ge(col_load.handle, COLS)
        dve.tensor_scalar(bias_n, bias, -1.0, None, ALU.mult).then_inc(bias_set.handle, 1)
        dve.wait_ge(bias_set.handle, 1)
        dve.tensor_scalar(bias, bias, 1.0, None, ALU.add).then_inc(bias_set.handle, 1)
        dve.tensor_tensor(gw_bo, gw, over(bo_col, E), ALU.mult).then_inc(bias_set.handle, 1)

    def set_from_constants(dve):
        dve.wait_ge(const_set.handle, CONSTS)
        dve.tensor_copy(spread, spread_f).then_inc(bias_set.handle, 1)
        dve.tensor_reduce(lo_rows, low.rearrange("p s g j -> p (s g j)"), AXX, ALU.add
                          ).then_inc(bias_set.handle, 1)
        dve.wait_ge(bias_set.handle, BIASES + 2)

    def set_gates(dve):
        dve.wait_ge(gate_sums.handle, 1)
        split_gates(dve, "wo_t", num_ps.rearrange("p g t -> p (g t)")[:, 0:KD * E].rearrange(
            "p (k e) -> p k e", e=EH), 1)
        dve.tensor_copy(g_sum, kv_ps[:, 0, 0:E]).then_inc(ready["wo_t"].handle, 1)
        dve.tensor_copy(g_bo, kv_ps[:, 0, E:2 * E]).then_inc(ready["wo_t"].handle, 1)
        dve.wait_ge(ready["wo_t"].handle, READY["wo_t"])

    def sum_gates(pe):
        pe.wait_ge(col_load.handle, COLS)
        pe.wait_ge(w_load["wo"].handle, 16)
        pe.wait_ge(bias_set.handle, BIASES)
        pe.wait_ge(const_set.handle, CONSTS)
        for k in range(KD):
            for f in range(KD):
                pe.matmul(num_ps[:, 0, k * E:(k + 1) * E], stages["wo"][:, f, k * P:(k + 1) * P],
                          gw[:, f, :], start=f == 0, stop=f == KD - 1)
        for m, g in enumerate((gw, gw_bo)):
            for f in range(KD):
                mm = pe.matmul(kv_ps[:, 0, m * E:(m + 1) * E], ones, g[:, f, :],
                               start=f == 0, stop=f == KD - 1)
        mm.then_inc(gate_sums.handle, 1)

    def set_identity(pool):
        pool.memset(neg_half, -0.5).then_inc(const_set.handle, 1)
        pool.memset(ident, 0.0).then_inc(const_set.handle, 1)
        pool.wait_ge(const_set.handle, 2)
        pool.affine_select(out=ident, in_=ident, compare_op=ALU.not_equal, fill=1.0, base=0,
                           pattern=[[-1, P]], channel_multiplier=1).then_inc(ident_set.handle, 1)

    def set_constants(pool):
        n = [2]

        def link(ins):
            ins.then_inc(const_set.handle, 1)
            n[0] += 1
            pool.wait_ge(const_set.handle, n[0])

        link(pool.memset(ones, 1.0))
        link(pool.memset(causal, 1.0))
        link(pool.affine_select(out=causal, in_=causal, compare_op=ALU.is_ge, fill=0.0, base=0,
                                pattern=[[1, P]], channel_multiplier=-1))
        link(pool.memset(diag_blocks, 1.0))
        v = diag_blocks.rearrange("p (j e) -> p j e", j=HPG)
        link(pool.affine_select(out=v, in_=v, compare_op=ALU.is_ge, fill=0.0, base=0,
                                pattern=[[-HD, HPG], [0, HD]], channel_multiplier=1))
        link(pool.affine_select(out=v, in_=v, compare_op=ALU.is_ge, fill=0.0, base=HD - 1,
                                pattern=[[HD, HPG], [0, HD]], channel_multiplier=-1))
        link(pool.memset(head_cols, 0.0))
        for s in range(2):
            for h in range(2):
                row = 2 * HPG * s + HPG * h
                link(pool.tensor_copy(head_cols[:, s, row:row + HPG], v[:, :, 0]))
        link(pool.memset(spread_f, 0.0))
        link(pool.memset(low, 0.0))
        for s in range(2):
            v = spread_f[:, s].rearrange("p g (j e) -> p g j e", j=HPG)
            for h in range(2):
                base = -(2 * HPG * s + HPG * h)
                link(pool.affine_select(out=v, in_=v, compare_op=ALU.not_equal, fill=1.0, base=base,
                                        pattern=[[-HD, KD], [-1, HPG], [0, HD]], channel_multiplier=1))
            link(pool.affine_select(out=low[:, s], in_=low[:, s], compare_op=ALU.not_equal, fill=-1.0,
                                    base=base, pattern=[[-HD, KD], [-1, HPG]], channel_multiplier=1))
        for e in range(E):
            link(pool.memset(order[:, e:e + 1], float(E - e)))
        assert n[0] == CONSTS
        pool.wait_ge(row_load.handle, ROWS)

    full = [sem(f"ring_full{k}") for k in range(NBANK)]
    free = [sem(f"ring_free{k}", CREDIT) for k in range(NBANK)]
    x_load = [sem(f"x_load{c}") for c in range(TPB)]
    res_load = [sem(f"res_load{n}") for n in range(2)]
    hi_parts, lo_parts = sem("hi_parts"), sem("lo_parts")
    cleared = sem("cleared")
    more_load = [sem(f"more_load{n}") for n in range(2)]
    stored = [sem(f"stored{n}", 16) for n in range(2)]
    x_stat, x_aggr, x_var, x_rstd, x_normed = (sem("x_stat"), sem("x_aggr"), sem("x_var"),
                                               sem("x_rstd"), sem("x_normed"))
    xt_hi, phi_relu, phi_exp = sem("xt_hi"), sem("phi_relu"), sem("phi_exp")
    k_scan, k_carried, prod = sem("k_scan"), sem("k_carried"), sem("prod")
    den_rec, rden_hi, rden_parts = sem("den_rec"), sem("rden_hi"), sem("rden_parts")
    scored, masked, summed = sem("scored", CREDIT), sem("masked", CREDIT), sem("summed")
    kv_done, kv_masked = sem("kv_done"), sem("kv_masked")
    o_hi, o_lo, res_bias = sem("o_hi"), sem("o_lo", CREDIT), sem("res_bias")
    x1_stat, x1_aggr = sem("x1_stat", CREDIT), sem("x1_aggr")
    gx_link, gx_done, z_link, z_done = sem("gx_link"), sem("gx_done"), sem("z_link"), sem("z_done", CREDIT)

    waited = {e.engine: sem(f"waited_{n}") for n, e in enumerate((nc.sync, nc.vector, nc.gpsimd))}

    def wait(eng, s, n):
        n = n + s.credit
        if not isinstance(n, int) or n > 0:
            eng.wait_ge(s.handle, n)
            if eng.engine == nc.sync.engine and not isinstance(n, int):
                eng.sem_inc(waited[eng.engine].handle, 1)

    def wait_alone(eng, s, n):
        wait(eng, s, n)
        if eng.engine != nc.sync.engine:
            eng.sem_inc(waited[eng.engine].handle, 1)

    def give(eng, *sems):
        for s in sems:
            eng.sem_inc(s.handle, s.credit)

    def wait_full(eng, st, u):
        k, n = st.use(u)
        wait(eng, full[k], n + 1)
        return ring[:, k, :]

    def wait_free(eng, st, u):
        k, n = st.use(u)
        wait(eng, free[k], n + 1)

    def wait_step_before(eng, st, *kinds):
        for k in sorted({BANK[u] for u in USES if u[0] in kinds}):
            wait(eng, free[k], st.before(k))

    def claim(pe, st, u):
        k, n = st.use(u)
        wait(pe, free[k], n)
        return ring[:, k, :]

    def done(sem_, ins):
        ins.then_inc(sem_.handle, 1)

    def filled(u, ins):
        done(full[BANK[u]], ins)

    def release(u, ins):
        done(free[BANK[u]], ins)

    loops = (n_blocks - 2) // 2
    base_m1 = per_bank(("turn",))
    base_0 = [a + b for a, b in zip(base_m1, per_bank(("proj", "turn")))]

    def base_at(t):
        return [a + b * t for a, b in zip(base_0, per_bank(ALL))]

    def run(eng, body, after_first=lambda: None):
        body(Step(0, -2, ("turn",), [0] * NBANK))
        after_first()
        body(Step(0, -1, ("proj", "turn"), base_m1))
        with eng.Fori(0, loops) as i:
            body(Step(i, 0, ALL, base_at(0)))
            body(Step(i, 1, ALL, base_at(1)))
        t = n_blocks - 2
        body(Step(0, t, ("attn", "proj"), base_at(t)))
        body(Step(0, t + 1, ("attn",), [a + b for a, b in zip(base_at(t), per_bank(("attn", "proj")))]))

    def kv_before(st, c):
        par = st.off % 2
        per = 2 * TPB - 1
        return st.i * per + (st.off // 2 * per + TPB * par + c)

    PAIR_ROWS = [slice(2 * HD * p, 2 * HD * (p + 1)) for p in range(2)]
    HIGHS, LOWS, MORES = 3 + HPG, 1 + HPG, 4 * 16

    def parts_count(st, per, off, c, h, n):
        return st.lin(per * 2 * TPB, off, per * (2 * c + h) + n)

    def first_tile(st, c):
        return st.off % 2 == 0 and c == 0

    def last_tile(st, c):
        return st.off % 2 == 1 and c == TPB - 1

    def phi_index(kind, g):
        return 2 * g + (kind == "K")

    chosen, exp_done, counted = sem("chosen"), sem("exp_done"), sem("counted")
    half = KD * BT // 2
    scratch = [buf.rearrange("p k t -> p (k t)")[:, h * half:(h + 1) * half] for buf in (x_in, k_sum)
               for h in range(2)]
    top_scratch = e_tmp[:, 0]
    assert n_blocks * TPB * E <= half and n_blocks * TPB <= BT
    PARTS = [(0, (n_blocks - 1) * TPB), ((n_blocks - 1) * TPB, n_blocks * TPB)]

    def part_steps(dve, m):
        a, b = PARTS[m]
        shape = [P, b - a, E]
        tiles = [s[:, 0:(b - a) * E].rearrange("p (t e) -> p t e", e=E) for s in scratch]
        return choosing(dve, z_all[:, a:b], order, count[:, m], shape, [*tiles, top_scratch[:, 0:b - a]],
                        chosen, m * CHOOSE_STEPS, lambda: wait(dve, exp_done, m + 1))

    def exponential(act, m):
        a, b = PARTS[m]
        wait(act, chosen, m * CHOOSE_STEPS + SHIFTED)
        done(exp_done, act.activation(z_all[:, a:b], z_all[:, a:b], ACT.Exp))

    block = ctx.enter_context(nc.Block())

    @block.sync
    def _(sp):
        def load_x(st):
            a = st.off + 2
            if a > 0:
                wait_step_before(sp, st, "X")
            for c in range(TPB):
                sp.dma_start(x_in[:, c, :], x_t[st.lin(TPB, a, c), :, :]).then_inc(x_load[c].handle, 16)

        def load_more(st, off, c, h):
            gs = slice(2 * h, 2 * h + 2)
            wait(sp, hi_parts, parts_count(st, HIGHS, off, c, h, HIGHS))
            for p in range(2):
                sp.dma_start(q_more.bitcast(F32)[PAIR_ROWS[1 - p], gs, p],
                             q_high.bitcast(F32)[PAIR_ROWS[p], gs, 2 * p:2 * p + 2]
                             ).then_inc(more_load[h].handle, 16)
            wait(sp, lo_parts, parts_count(st, LOWS, off, c, h, 1))
            for p in range(2):
                sp.dma_start(k_more.bitcast(F32)[PAIR_ROWS[1 - p], gs, p],
                             k_low.bitcast(F32)[PAIR_ROWS[p], gs]).then_inc(more_load[h].handle, 16)

        def load_res(st, off, c):
            if not (off == 0 and c < 2 and isinstance(st.i, int)):
                wait(sp, stored[c % 2], st.lin(TPB // 2 * 16, off, c // 2 * 16))
                wait_alone(sp, x1_stat, st.lin(TPB, off, c - 1))
            sp.dma_start(res[:, c % 2, :], x_t[st.lin(TPB, off, c), :, :]
                         ).then_inc(res_load[c % 2].handle, 16)

        def store(st, c):
            k, n = st.use(("O", (c, 1)))
            wait_alone(sp, free[k], n + 1)
            sp.dma_start(out_t[st.lin(TPB, st.off, c), :, :], res[:, c % 2, :]
                         ).then_inc(stored[c % 2].handle, 16)

        def body(st):
            t = st.off
            if not st.has("attn"):
                load_x(st)
                if st.has("proj"):
                    load_res(st, t + 1, 0)
                    for h in range(2):
                        load_more(st, t + 1, 0, h)
                return
            for c in range(TPB):
                last = c == TPB - 1
                nxt = (t + 1, 0) if last else (t, c + 1)
                if c == 0 and st.has("turn"):
                    load_x(st)
                if not last or st.has("proj"):
                    for h in range(2):
                        load_more(st, *nxt, h)
                if not st.has("proj") and c:
                    store(st, c - 1)
                if not last or st.has("proj"):
                    load_res(st, *nxt)
                if st.has("proj") or last:
                    store(st, c)

        give(sp, *stored)
        run(sp, body, lambda: load_weights(sp))
        for s in stored:
            wait(sp, s, n_blocks * TPB // 2 * 16)

    @block.tensor
    def _(pe):
        def turn(st, c):
            u = ("X", c)
            bank = claim(pe, st, u)
            wait(pe, x_normed, st.lin(TPB, st.off + 2, c + 1))
            for k in range(KD):
                mm = pe.transpose(bank[:, k * P:(k + 1) * P], x_in[:, c, k * P:(k + 1) * P], ident)
            filled(u, mm)

        def project(st, kind, g):
            u = (kind, g)
            w = w_q if kind == "Q" else w_k
            bank = claim(pe, st, u)
            n = 0
            for k in range(KD):
                for a, b in ((0, 0), (0, 1), (1, 0)):
                    mm = pe.matmul(bank, w[a][:, k, g * P:(g + 1) * P], xt[b][:, k, :],
                                   start=n == 0, stop=n == 3 * KD - 1)
                    n += 1
            filled(u, mm)

        def two_halves(st, kind, c, rows, w):
            for h in range(2):
                u = (kind, (c, h))
                bank = claim(pe, st, u)
                n = 0
                for k in range(KD):
                    for a, b in ((0, 0), (0, 1), (1, 0)):
                        mm = pe.matmul(bank[:, 0:HW], rows[a](k), w[b][:, k, h, :],
                                       start=n == 0, stop=n == 3 * KD - 1)
                        n += 1
                filled(u, mm)

        def chunk(st, c, m):
            for kind, j in CHUNKS[c, m]:
                if j == 0 and not st.has("attn"):
                    name = f"w{kind.lower()}_t"
                    wait(pe, ready[name], READY[name])
                if kind != "V":
                    project(st, kind, j)
                else:
                    two_halves(st, "V", j, [lambda k, h=h: xt[h][:, k, j * P:(j + 1) * P] for h in range(2)], w_v)

        def denominators(st):
            u = ("DEN", 0)
            bank = claim(pe, st, u)
            wait(pe, prod, st.lin(KD, st.off + 1, KD))
            for g in range(KD):
                for s in range(2):
                    mm = pe.matmul(bank[g * HD:(g + 1) * HD, 0:BT // 2], head_cols[:, s],
                                   k_sum[:, g, s * BT // 2:(s + 1) * BT // 2], start=s == 0, stop=s == 1,
                                   tile_position=(0, g * HD))
            filled(u, mm)

        def spread_reciprocals(st, groups):
            if groups[0] == 0:
                wait(pe, rden_parts, st.lin(1, st.off + 1, 1))
            for g in groups:
                u = ("R", g)
                bank = claim(pe, st, u)
                for s in range(2):
                    mm = pe.matmul(bank[:, s * BT // 2:(s + 1) * BT // 2], spread[:, s, g, :], rden,
                                   start=True, stop=True)
                filled(u, mm)

        def scores(st, c, g):
            idx = st.lin(TPB * KD, st.off, c * KD + g)
            wait(pe, masked, idx - 1)
            if g % 2 == 0:
                wait(pe, lo_parts, parts_count(st, LOWS, st.off, c, g // 2, LOWS))
                wait(pe, more_load[g // 2], st.lin(TPB * MORES, st.off, (c + 1) * MORES))
            pe.matmul(s_ps[:, g % 2], k_high[:, g], q_high[:, g], start=True, stop=False, skip_group_check=True)
            for p in range(2):
                mm = pe.matmul(s_ps[:, g % 2, 2 * p:2 * p + 2], k_more[:, g, p], q_more[:, g, p],
                               start=False, stop=p == 1, skip_group_check=True)
            done(scored, mm)

        def turn_keys(st, c):
            u = ("T", c)
            bank = claim(pe, st, u)
            for g in range(KD):
                mm = pe.transpose(bank[:, g * P:(g + 1) * P], k_t[:, st.off % 2, g, c * P:(c + 1) * P], ident)
            filled(u, mm)

        def start_tile(st, c):
            scores(st, c, 0)
            scores(st, c, 1)
            turn_keys(st, c)

        def from_state(st, c):
            wait(pe, o_lo, st.lin(TPB, st.off, c))
            if first_tile(st, c):
                return
            wait(pe, kv_masked, kv_before(st, c))
            for g in range(KD):
                pe.matmul(num_ps[:, g], kv_diag[:, g], q_div[:, g, c * P:(c + 1) * P],
                          start=g == 0, stop=False, skip_group_check=True)

        def from_tile(st, c, g):
            wait(pe, masked, st.lin(TPB * KD, st.off, c * KD + g + 1))
            for j in range(HPG):
                col = (g * HPG + j) * HD
                mm = pe.matmul(num_ps[j * HD:(j + 1) * HD, g], v_tok[:, c, col:col + HD],
                               s_mask[:, g % 2, j], start=first_tile(st, c) and g == 0,
                               stop=g == KD - 1, skip_group_check=True, tile_position=(0, j * HD))
            if g == KD - 1:
                done(summed, mm)

        def add_state(st, c):
            if last_tile(st, c):
                return
            wait_free(pe, st, ("T", c))
            for g in range(KD):
                mm = pe.matmul(kv_ps[:, g], k_tok[:, g * P:(g + 1) * P], v_tok[:, c, g * P:(g + 1) * P],
                               start=first_tile(st, c) and g == 0, stop=g == KD - 1, skip_group_check=True)
            done(kv_done, mm)

        def body(st):
            attn, proj, turns = (st.has(p) for p in ALL)
            if not attn and not proj:
                for c in range(TPB):
                    turn(st, c)
                return
            for c in range(TPB):
                last = c == TPB - 1
                if last and proj:
                    denominators(st)
                if attn and (proj or c == 0):
                    start_tile(st, c)
                if last and turns:
                    turn(st, 0)
                if c == 1 and not attn:
                    sum_gates(pe)
                if proj:
                    if c == 0:
                        wait_step_before(pe, st, "X")
                    chunk(st, c, 0)
                if last and turns:
                    turn(st, 1)
                if attn:
                    if c == 0:
                        wait_step_before(pe, st, "V")
                    from_state(st, c)
                    from_tile(st, c, 0)
                    scores(st, c, 2)
                    from_tile(st, c, 1)
                    scores(st, c, 3)
                    add_state(st, c)
                if proj:
                    if last:
                        spread_reciprocals(st, (0, 1))
                    chunk(st, c, 1)
                if attn:
                    from_tile(st, c, 2)
                    from_tile(st, c, 3)
                if last and proj:
                    spread_reciprocals(st, (2, 3))
                if last and turns:
                    turn(st, 2)
                if proj:
                    chunk(st, c, 2)
                if last and turns:
                    turn(st, 3)
                if not proj and not last:
                    start_tile(st, c + 1)
                if attn:
                    wait(pe, o_lo, st.lin(TPB, st.off, c + 1))
                    two_halves(st, "O", c, [lambda k, h=h: o_t[h][:, k, :] for h in range(2)], w_o)

        give(pe, scored)
        pe.wait_ge(ident_set.handle, 1)
        run(pe, body)
        wait(pe, chosen, 2 * CHOOSE_STEPS)
        for m in range(2):
            mm = pe.matmul(ring[:, 0, 0:E], ones, count[:, m], start=m == 0, stop=m == 1)
        done(counted, mm)

    @block.scalar
    def _(act):
        def relu_exp(st, kind, g):
            u, m = (kind, g), kind == "K"
            bank = wait_full(act, st, u)
            if g:
                wait_free(act, st, (kind, g - 1))
            else:
                wait_step_before(act, st, kind)
            n = st.lin(2 * KD, st.off + 1, phi_index(kind, g) + 1)
            done(phi_relu, act.activation(e_tmp[:, m], bank, ACT.Relu, bias=bias_n[:, m, g:g + 1], scale=-1.0))
            wait(act, phi_relu, n)
            done(phi_exp, act.activation(e_tmp[:, m], e_tmp[:, m], ACT.Exp, scale=-1.0))

        def turn_hi(st, c):
            bank = wait_full(act, st, ("X", c))
            done(xt_hi, act.activation(xt[0][:, :, c * P:(c + 1) * P], bank.rearrange("p (k t) -> p k t", k=KD),
                                       ACT.Copy))

        def chunk(st, c, m):
            for kind, j in CHUNKS[c, m]:
                if kind != "V":
                    relu_exp(st, kind, j)

        def high_parts(st, off, c, h):
            gs, t = slice(2 * h, 2 * h + 2), slice(c * P, (c + 1) * P)
            wait(act, scored, st.lin(TPB * KD, off, (c - 1) * KD + 2 * h + 2))
            k = k_t[:, off % 2, gs, t]
            done(hi_parts, act.activation(k_high[:, gs], k, ACT.Copy))
            for p, rows in enumerate(PAIR_ROWS):
                done(hi_parts, act.activation(k_more[rows, gs, p], k[rows], ACT.Copy))
            if off > st.off:
                wait_free(act, st, ("R", 2 * h + 1))
            for j in range(HPG):
                rows = slice(HD * j, HD * (j + 1))
                done(hi_parts, act.activation(q_high[rows, gs, j], q_div[rows, gs, t], ACT.Copy))

        def next_high(st, c, h):
            if c < TPB - 1:
                if st.has("attn"):
                    high_parts(st, st.off, c + 1, h)
            elif st.has("proj"):
                high_parts(st, st.off + 1, 0, h)

        def body(st):
            attn, proj, turns = (st.has(p) for p in ALL)
            if not attn and not proj:
                for c in range(TPB):
                    turn_hi(st, c)
                return
            for c in range(TPB):
                last = c == TPB - 1
                if last and proj:
                    u = ("DEN", 0)
                    release(u, act.activation(den, wait_full(act, st, u)[:, 0:BT // 2], ACT.Copy,
                                              bias=DEN_EPS))
                if attn:
                    u = ("T", c)
                    release(u, act.activation(k_tok, wait_full(act, st, u), ACT.Copy))
                if last and turns:
                    turn_hi(st, 0)
                if c in (1, 2) and not attn:
                    split_high(act, ("wv_t", "wo_t")[c - 1])
                if c == 0 and not attn:
                    wait(act, cleared, 2)
                if proj:
                    chunk(st, c, 0)
                if last and turns:
                    turn_hi(st, 1)
                if last and proj:
                    wait(act, den_rec, st.lin(1, st.off + 1, 1))
                    done(rden_hi, act.activation(rden_high, den, ACT.Copy))
                next_high(st, c, 0)
                if proj:
                    chunk(st, c, 1)
                if c == 0 and not proj:
                    exponential(act, 0)
                if attn:
                    wait(act, summed, st.lin(TPB, st.off, c + 1))
                    done(o_hi, act.activation(o_t[0], num_ps, ACT.Copy))
                if last and turns:
                    turn_hi(st, 2)
                next_high(st, c, 1)
                if proj:
                    chunk(st, c, 2)
                if last and turns:
                    turn_hi(st, 3)

        def split_first():
            split_high(act, "wk_t")
            act.wait_ge(bias_set.handle, BIASES)

        load_biases(act)
        split_high(act, "wq_t")
        run(act, body, split_first)
        exponential(act, 1)

    @block.vector
    def _(dve):
        def mask_scores(st, c, g):
            idx = st.lin(TPB * KD, st.off, c * KD + g)
            wait(dve, scored, idx + 1)
            done(masked, dve.tensor_tensor(s_mask[:, g % 2], s_ps[:, g % 2], repeat(causal, HPG), ALU.mult))

        def mask_state(st, c):
            if not last_tile(st, c):
                wait(dve, kv_done, kv_before(st, c) + 1)
                done(kv_masked, dve.tensor_tensor(kv_diag, kv_ps, repeat(diag_blocks, KD), ALU.mult))

        def phi(st, kind, g):
            u, m = (kind, g), kind == "K"
            bank = wait_full(dve, st, u)
            wait(dve, phi_exp, st.lin(2 * KD, st.off + 1, phi_index(kind, g) + 1))
            par = (st.off + 1) % 2
            out = k_t[:, par, g] if m else q_raw[:, g]
            release(u, dve.scalar_tensor_tensor(out, bank, bias[:, m, g:g + 1], e_tmp[:, m], ALU.add, ALU.max))

        def key_sums(st, g):
            par = (st.off + 1) % 2
            out = k_t[:, par, g]
            n = st.lin(KD, st.off + 1, g + 1)
            wait_free(dve, st, ("K", g))
            start = 0.0 if par == 0 else k_carry[:, g:g + 1]
            done(k_scan, dve.tensor_tensor_scan(k_sum[:, g], out, out, start, ALU.add, ALU.max))
            wait(dve, k_scan, n)
            done(k_carried, dve.tensor_copy(k_carry[:, g:g + 1], k_sum[:, g, BT - 1:BT]))

        def values(st, c):
            for h in range(2):
                u = ("V", (c, h))
                bank = wait_full(dve, st, u)
                dve.tensor_tensor(v_tok[:, c, h * DH:(h + 1) * DH], bank[:, 0:DH],
                                  bv_row[:, h * DH:(h + 1) * DH], ALU.add)
                release(u, dve.tensor_copy(gate_x[:, (st.off + 1) % 2, c, h * EH:(h + 1) * EH], bank[:, DH:HW]))

        def chunk(st, c, m):
            for kind, j in CHUNKS[c, m]:
                values(st, j) if kind == "V" else phi(st, kind, j)

        def chunk_sums(st, c, m):
            for kind, j in CHUNKS[c, m]:
                if kind == "K":
                    key_sums(st, j)

        def divide(st, groups):
            for g in groups:
                u = ("R", g)
                bank = wait_full(dve, st, u)
                release(u, dve.tensor_tensor(q_div[:, g], bank, q_raw[:, g], ALU.mult))

        def turn_lo(st, c):
            u = ("X", c)
            bank = wait_full(dve, st, u).rearrange("p (k t) -> p k t", k=KD)
            wait(dve, xt_hi, st.lin(TPB, st.off + 2, c + 1))
            t = slice(c * P, (c + 1) * P)
            release(u, dve.tensor_tensor(xt[1][:, :, t], bank, xt[0].bitcast(F32)[:, :, t], ALU.subtract))

        def moments(st, tiles):
            a = st.off + 2
            for c in tiles:
                wait(dve, x_load[c], st.lin(16, a, 16))
                done(x_stat, dve.bn_stats(stats[:, c], x_in[:, c]))
            if tiles[0] == 0:
                wait(dve, gx_done, st.lin(1, a - 1))
            for c in tiles:
                wait_alone(dve, x_stat, st.lin(TPB, a, c + 1))
                done(x_aggr, dve.bn_aggr(mv0[:, a % 2, c], stats[:, c]))

        def normalise(st, c):
            a = st.off + 2
            if c == 0:
                wait(dve, x_rstd, st.lin(1, a, 1))
            done(x_normed, dve.tensor_scalar(x_in[:, c], x_in[:, c], mv0[:, a % 2, c, 0:1],
                                             rstd0[:, a % 2, c:c + 1], ALU.subtract, ALU.mult))

        def residual(st, c):
            if c == 0:
                wait(dve, z_done, st.lin(1, st.off))
            wait(dve, res_bias, st.lin(TPB, st.off, c + 1))
            for h in range(2):
                u = ("O", (c, h))
                bank = wait_full(dve, st, u)
                cols = slice(h * DH, (h + 1) * DH)
                dve.tensor_tensor(res[:, c % 2, cols], bank[:, 0:DH], res[:, c % 2, cols], ALU.add)
                release(u, dve.tensor_tensor(gate_o[:, c, h * EH:(h + 1) * EH], bank[:, DH:HW],
                                             g_bo[:, h * EH:(h + 1) * EH], ALU.add))
            wait_free(dve, st, ("O", (c, 1)))
            done(x1_stat, dve.bn_stats(stats1[:, c], res[:, c % 2]))
            wait_alone(dve, x1_stat, st.lin(TPB, st.off, c + 1))
            done(x1_aggr, dve.bn_aggr(mv1[:, c], stats1[:, c]))

        def body(st):
            attn, proj, turns = (st.has(p) for p in ALL)
            if not attn:
                moments(st, range(TPB))
            if not attn and not proj:
                for c in range(TPB):
                    normalise(st, c)
                for c in range(TPB):
                    turn_lo(st, c)
                return
            for c in range(TPB):
                last = c == TPB - 1
                if attn and (proj or c == 0):
                    mask_scores(st, c, 0)
                    mask_scores(st, c, 1)
                if last and proj:
                    wait_free(dve, st, ("DEN", 0))
                    done(den_rec, dve.reciprocal(den, den))
                if last and turns:
                    turn_lo(st, 0)
                if c == 1 and not attn:
                    split_low(dve, "wv_t")
                    split_gates(dve, "wv_t", gw.rearrange("p k (h e) -> p (k h) e", h=2), 0)
                if c == 2 and not attn:
                    split_low(dve, "wo_t")
                    set_gates(dve)
                if proj:
                    chunk(st, c, 0)
                    chunk_sums(st, c, 0)
                if last and proj:
                    wait(dve, rden_hi, st.lin(1, st.off + 1, 1))
                    done(rden_parts, dve.scalar_tensor_tensor(rden, rden_high.bitcast(F32), lo_rows, den,
                                                              ALU.mult, ALU.add))
                if last and turns:
                    turn_lo(st, 1)
                if attn:
                    mask_scores(st, c, 2)
                    mask_scores(st, c, 3)
                    mask_state(st, c)
                    if c == 0 and not proj:
                        wait(dve, z_done, st.lin(1, st.off))
                        choose_more(SHIFTED)
                    if c == 1 and turns:
                        moments(st, (0, 1))
                if last and proj:
                    divide(st, (0, 1))
                if proj:
                    chunk(st, c, 1)
                if last and proj:
                    divide(st, (2, 3))
                if attn:
                    wait(dve, o_hi, st.lin(TPB, st.off, c + 1))
                    done(o_lo, dve.tensor_tensor(o_t[1], num_ps, o_t[0].bitcast(F32), ALU.subtract))
                if last and turns:
                    turn_lo(st, 2)
                if proj:
                    chunk_sums(st, c, 1)
                if c == 1 and attn and turns:
                    moments(st, (2, 3))
                if proj:
                    chunk(st, c, 2)
                    chunk_sums(st, c, 2)
                if c == 2 and turns:
                    for a in range(TPB):
                        normalise(st, a)
                if last and turns:
                    turn_lo(st, 3)
                if not proj:
                    if not last:
                        mask_scores(st, c + 1, 0)
                        mask_scores(st, c + 1, 1)
                        choose_more(3)
                    else:
                        choose_more(1)
                if attn:
                    residual(st, c)
                if not proj:
                    choose_more(2)

        def set_first():
            set_biases(dve)
            split_low(dve, "wq_t")
            split_low(dve, "wk_t")
            set_from_constants(dve)
            dve.wait_ge(row_load.handle, ROWS)

        give(dve, *free, masked, o_lo, x1_stat)
        first_part = part_steps(dve, 0)

        def choose_more(n):
            for step in first_part[:n]:
                step()
            del first_part[:n]

        run(dve, body, set_first)
        assert not first_part
        wait(dve, z_done, n_blocks)
        for step in part_steps(dve, 1):
            step()
        wait(dve, counted, 1)
        done(chosen, dve.tensor_scalar(keep, ring[:, 0, 0:E], float(capacity), None, ALU.is_le))
        wait(dve, chosen, 2 * CHOOSE_STEPS + 1)
        dve.tensor_reduce(any_kept, keep, AXX, ALU.max)

    @block.gpsimd
    def _(pool):
        def rstds(st):
            a = st.off + 2
            wait_alone(pool, x_aggr, st.lin(TPB, a, TPB))
            done(x_var, pool.tensor_scalar(var0[:, a % 2], mv0[:, a % 2, :, 1], LN_EPS, None, ALU.add))
            wait(pool, x_var, st.lin(1, a, 1))
            done(x_rstd, pool.tensor_tensor(rstd0[:, a % 2], var0[:, a % 2], neg_half, ALU.pow))

        def products(st, g):
            wait(pool, k_carried, st.lin(KD, st.off + 1, g + 1))
            done(prod, pool.tensor_tensor(k_sum[:, g], k_sum[:, g], q_raw[:, g], ALU.mult))

        def linked(s, st, off, per):
            n = [0]

            def link(ins):
                n[0] += 1
                done(s, ins)
                wait(pool, s, st.lin(per, off, n[0]))
            return link

        def gate_in(st):
            b = (st.off + 1) % 2
            link = linked(gx_link, st, st.off + 1, 3)
            wait_free(pool, st, ("V", (TPB - 1, 1)))
            wait_free(pool, st, ("V", (TPB - 1, 0)))
            link(pool.tensor_tensor(std0, var0[:, b], rstd0[:, b], ALU.mult))
            link(pool.tensor_tensor(gate_x[:, b], gate_x[:, b], over(std0, E), ALU.mult))
            link(pool.tensor_tensor(z_a, repeat(g_sum, TPB), over(mv0[:, b, :, 0:1], E), ALU.mult))
            done(gx_done, pool.tensor_tensor(gate_x[:, b], gate_x[:, b], z_a, ALU.add))

        def logits(st):
            b = st.off % 2
            link = linked(z_link, st, st.off, 6)
            wait_free(pool, st, ("O", (TPB - 1, 1)))
            wait(pool, x1_aggr, st.lin(TPB, st.off, TPB))
            wait_alone(pool, gx_done, st.lin(1, st.off, 1))
            link(pool.tensor_scalar(var1, mv1[:, :, 1], LN_EPS, None, ALU.add))
            link(pool.tensor_tensor(rstd1, var1, neg_half, ALU.pow))
            link(pool.tensor_tensor(z_b, repeat(g_sum, TPB), over(mv1[:, :, 0:1], E), ALU.mult))
            link(pool.tensor_tensor(z_b, gate_x[:, b], z_b, ALU.subtract))
            link(pool.tensor_tensor(z_b, z_b, gate_o, ALU.add))
            tiles = st.lin(TPB, st.off)
            link(pool.tensor_tensor(z_all[:, bass.ds(tiles, TPB), :], z_b, over(rstd1, E), ALU.mult))
            done(z_done, pool.tensor_copy(keepers["moments"][:, bass.ds(tiles, TPB), 0:1], mv1[:, :, 0:1]))
            pool.tensor_copy(keepers["moments"][:, bass.ds(tiles, TPB), 1:2], rstd1.unsqueeze(2))

        def chunk(st, c, m):
            for kind, j in CHUNKS[c, m]:
                if kind == "K":
                    products(st, j)

        def low_parts(st, off, c, h):
            gs, t = slice(2 * h, 2 * h + 2), slice(c * P, (c + 1) * P)
            wait(pool, hi_parts, parts_count(st, HIGHS, off, c, h, 1))
            done(lo_parts, pool.tensor_tensor(k_low[:, gs], k_t[:, off % 2, gs, t],
                                              k_high.bitcast(F32)[:, gs], ALU.subtract))
            wait(pool, hi_parts, parts_count(st, HIGHS, off, c, h, HIGHS))
            for j in range(HPG):
                wait(pool, lo_parts, parts_count(st, LOWS, off, c, h, 1 + j))
                rows = slice(HD * j, HD * (j + 1))
                done(lo_parts, pool.tensor_tensor(q_more[rows, gs, j // 2, j % 2], q_div[rows, gs, t],
                                                  q_high.bitcast(F32)[rows, gs, j], ALU.subtract))
            wait(pool, lo_parts, parts_count(st, LOWS, off, c, h, LOWS))

        def next_low(st, c, h):
            if c < TPB - 1:
                if st.has("attn"):
                    low_parts(st, st.off, c + 1, h)
            elif st.has("proj"):
                low_parts(st, st.off + 1, 0, h)

        def body(st):
            attn, proj, turns = (st.has(p) for p in ALL)
            if not attn and not proj:
                rstds(st)
                return
            for c in range(TPB):
                last = c == TPB - 1
                if proj:
                    chunk(st, c, 0)
                next_low(st, c, 0)
                if attn:
                    wait(pool, res_load[c % 2], st.lin(TPB // 2 * 16, st.off, (c // 2 + 1) * 16))
                    done(res_bias, pool.tensor_tensor(res[:, c % 2], res[:, c % 2], bo_row, ALU.add))
                if c == 1 and turns:
                    rstds(st)
                if proj:
                    chunk(st, c, 1)
                next_low(st, c, 1)
                if proj:
                    chunk(st, c, 2)
                if last and proj:
                    gate_in(st)
                if last and attn:
                    logits(st)

        def set_rest():
            set_constants(pool)
            done(cleared, pool.memset(q_more.bitcast(F32), 0.0))
            done(cleared, pool.memset(q_high.bitcast(F32), 0.0))

        give(pool, z_done)
        set_identity(pool)
        run(pool, body, set_rest)
def experts(nc, io, n_blocks, keepers):
    wts, keep, any_kept, moments, ident = (keepers[n] for n in ("z_all", "keep", "any_kept", "moments", "ident"))
    out_b = io["out"].rearrange("(n c p) d -> n p c d", c=TPB, p=P)
    with ExitStack() as ctx:
        def sb(name, shape, dt=F32):
            return ctx.enter_context(nc.sbuf_tensor(name, shape, dt))[:]

        def sem(name, credit=0):
            return Sem(ctx.enter_context(nc.semaphore(name)), credit)

        w1 = sb("e_w1", [P, 2, KD, D])
        w2 = sb("e_w2", [P, 2, KD, D])
        b1 = sb("e_b1", [P, 2, KD])
        b2 = sb("e_b2", [P, 2, D])
        acc = sb("e_acc", [P, TPB, D])
        norm = sb("e_norm", [P, TPB, D])
        mom = sb("e_mom", [P, TPB, 2])
        wt = sb("e_wt", [P, TPB, E])
        xt = sb("e_xt", [P, KD, BT])
        hid = sb("e_hid", [P, KD, BT])
        y_b = sb("e_y", [P, D])
        pt = ctx.enter_context(nc.psum_tensor("e_pt", [P, TPB, 512], F32))[:]
        ph = ctx.enter_context(nc.psum_tensor("e_ph", [P, 2, 512], F32))[:]
        py = ctx.enter_context(nc.psum_tensor("e_py", [P, 2, 512], F32))[:]

        x1_load, w_load = sem("e_x1_load"), [sem(f"e_w_load{n}") for n in range(2)]
        copied, normed = sem("e_copied"), sem("e_normed")
        turned, turned_out = sem("e_turned"), sem("e_turned_out", CREDIT)
        h_full, h_out = sem("e_h_full"), sem("e_h_out", CREDIT)
        y_full, y_bias, y_added = sem("e_y_full"), sem("e_y_bias"), sem("e_y_added", 2 * TPB)
        out_store, passed = sem("e_out_store", 16), {e.engine: sem(f"e_passed{n}") for n, e in
                                                     enumerate((nc.sync, nc.vector))}

        def wait(eng, s, n):
            eng.wait_ge(s.handle, n + s.credit)
            if eng.engine in passed:
                eng.sem_inc(passed[eng.engine].handle, 1)

        def done(s, ins):
            ins.then_inc(s.handle, 1)

        def give(eng, *sems):
            for s in sems:
                eng.sem_inc(s.handle, s.credit)

        def over_experts(eng, i, body):
            with eng.Fori(0, E // 2) as j:
                for n in range(2):
                    body(n, i * (E // 2) + j + 1, j * 2 + n, i * E + j * 2 + n)

        block = ctx.enter_context(nc.Block())

        def where_kept(eng, body):
            flag = eng.value_load(any_kept[0:1, 0:1], min_val=0, max_val=1)
            with eng.If(flag > 0):
                with eng.Fori(0, n_blocks) as i:
                    body(i)

        @block.sync
        def _(sp):
            def body(i):
                wait(sp, out_store, i * 16)
                sp.dma_start(acc, out_b[i, :, :, :]).then_inc(x1_load.handle, 16)

                def load(n, uses, e, idx):
                    wait(sp, y_added, (idx - 1) * TPB)
                    for dst, src in ((w1[:, n], io["w1_t"]), (w2[:, n], io["w2_t"])):
                        sp.dma_start(dst, src[e, :, :].rearrange("(k p) d -> p k d", p=P)
                                     ).then_inc(w_load[n].handle, 16)
                    with nc.allow_non_contiguous_dma("a column of biases"):
                        sp.dma_start(b1[:, n], io["b1"][e, :].rearrange("(k p) -> p k", p=P)
                                     ).then_inc(w_load[n].handle, 16)
                    sp.dma_start(b2[:, n], io["b2"][bass.ds(e, 1), :].to_broadcast([P, D])
                                 ).then_inc(w_load[n].handle, 16)
                over_experts(sp, i, load)
                wait(sp, y_added, (i + 1) * (E * TPB))
                sp.dma_start(out_b[i, :, :, :], acc).then_inc(out_store.handle, 16)

            give(sp, out_store)
            where_kept(sp, body)
            flag = sp.value_load(any_kept[0:1, 0:1], min_val=0, max_val=1)
            with sp.If(flag > 0):
                sp.wait_ge(out_store.handle, (n_blocks + 1) * 16)

        @block.vector
        def _(dve):
            def body(i):
                tiles = bass.ds(i * TPB, TPB)
                wait(dve, x1_load, (i + 1) * 16)
                done(copied, dve.tensor_copy(mom, moments[:, tiles, :]))
                done(copied, dve.tensor_tensor(wt, wts[:, tiles, :], keep.unsqueeze(1).to_broadcast([P, TPB, E]),
                                               ALU.mult))
                wait(dve, copied, (i + 1) * 2)
                for c in range(TPB):
                    done(normed, dve.tensor_scalar(norm[:, c], acc[:, c], mom[:, c, 0:1], mom[:, c, 1:2],
                                                   ALU.subtract, ALU.mult))

                def add(n, uses, e, idx):
                    for c in range(TPB):
                        m = idx * TPB + c
                        wait(dve, y_full, m + 1)
                        wait(dve, y_added, m)
                        done(y_bias, dve.tensor_tensor(y_b, py[:, c % 2], b2[:, n], ALU.add))
                        wait(dve, y_bias, m + 1)
                        done(y_added, dve.scalar_tensor_tensor(acc[:, c], y_b, wt[:, c, bass.ds(e, 1)], acc[:, c],
                                                               ALU.mult, ALU.add))
                over_experts(dve, i, add)

            give(dve, y_added)
            where_kept(dve, body)

        @block.tensor
        def _(pe):
            def body(i):
                for c in range(TPB):
                    wait(pe, normed, i * TPB + c + 1)
                    if c == 0:
                        wait(pe, turned_out, i * TPB)
                    for k in range(KD):
                        mm = pe.transpose(pt[:, c, k * P:(k + 1) * P], norm[:, c, k * P:(k + 1) * P], ident)
                    done(turned, mm)

                def expert(n, uses, e, idx):
                    for g in range(KD):
                        wait(pe, h_out, idx * KD + g - 1)
                        if g == 0:
                            wait(pe, w_load[n], uses * 64)
                            wait(pe, turned_out, (i + 1) * TPB)
                        for k in range(KD):
                            mm = pe.matmul(ph[:, g % 2], w1[:, n, k, g * P:(g + 1) * P], xt[:, k],
                                           start=k == 0, stop=k == KD - 1)
                        done(h_full, mm)
                    wait(pe, h_out, (idx + 1) * KD)
                    for c in range(TPB):
                        wait(pe, y_added, idx * TPB + c - 1)
                        for g in range(KD):
                            mm = pe.matmul(py[:, c % 2], hid[:, g, c * P:(c + 1) * P], w2[:, n, g],
                                           start=g == 0, stop=g == KD - 1)
                        done(y_full, mm)
                over_experts(pe, i, expert)

            where_kept(pe, body)

        @block.scalar
        def _(act):
            def body(i):
                for c in range(TPB):
                    wait(act, turned, i * TPB + c + 1)
                    done(turned_out, act.activation(xt[:, :, c * P:(c + 1) * P],
                                                    pt[:, c].rearrange("p (k t) -> p k t", k=KD), ACT.Copy))

                def hidden(n, uses, e, idx):
                    for g in range(KD):
                        wait(act, h_full, idx * KD + g + 1)
                        done(h_out, act.activation(hid[:, g], ph[:, g % 2], ACT.Silu, bias=b1[:, n, g:g + 1]))
                over_experts(act, i, hidden)

            give(act, turned_out, h_out)
            where_kept(act, body)


def program(nc, io, n_tok):
    n_tiles = n_tok // P
    with ExitStack() as keep:
        def sb(name, shape, dt=F32):
            return keep.enter_context(nc.sbuf_tensor(name, shape, dt))[:]

        keepers = {"z_all": sb("z_all", [P, n_tiles, E]), "moments": sb("moments", [P, n_tiles, 2]),
                   "ident": sb("ident", [P, P]), "ones": sb("ones", [P, P]),
                   "keep": sb("keep", [P, E]), "any_kept": sb("any_kept", [P, 1], I32)}
        with ExitStack() as ctx:
            attention(nc, ctx, io, n_tok // BT, keepers, int(CAPACITY_FACTOR * n_tok / E))
        nc.all_engine_barrier()
        experts(nc, io, n_tok // BT, keepers)


def kernel(L0_attn_x, L0_attn_Wq, L0_attn_bq, L0_attn_Wk, L0_attn_bk, L0_attn_Wv, L0_attn_bv, L0_attn_Wo,
           L0_attn_bo, L0_ffn_gate_w, L0_ffn_w1, L0_ffn_b1, L0_ffn_w2, L0_ffn_b2):
    import concourse.bacc as bacc
    from concourse.bass_utils import run_bass_kernel_spmd

    x = np.asarray(L0_attn_x)
    n_tok = x.shape[0] * x.shape[1]
    arrays = {"x": x.reshape(n_tok, D), "wq_t": np.asarray(L0_attn_Wq).T, "wk_t": np.asarray(L0_attn_Wk).T,
              "wv_t": np.asarray(L0_attn_Wv).T, "wo_t": np.asarray(L0_attn_Wo).T, "wo": np.asarray(L0_attn_Wo),
              "bq": L0_attn_bq, "bk": L0_attn_bk, "bv": L0_attn_bv, "bo": L0_attn_bo,
              "gate": np.asarray(L0_ffn_gate_w).T,
              "w1_t": np.asarray(L0_ffn_w1).transpose(0, 2, 1), "b1": L0_ffn_b1,
              "w2_t": np.asarray(L0_ffn_w2).transpose(0, 2, 1), "b2": L0_ffn_b2}
    arrays = {f"in_{name}": np.ascontiguousarray(a) for name, a in arrays.items()}

    nc = bacc.Bacc("TRN2", target_bir_lowering=False, num_devices=1)
    io = {name[3:]: nc.dram_tensor(name, a.shape, mybir.dt.from_np(a.dtype), kind="ExternalInput").ap()
          for name, a in arrays.items()}
    io["out"] = nc.dram_tensor("out", (n_tok, D), F32, kind="ExternalOutput").ap()
    program(nc, io, n_tok)
    results = run_bass_kernel_spmd(nc, [arrays], core_ids=[0])
    return results.results[0]["out"].reshape(x.shape)
```
